# Optimizing a Trainium2 kernel written in Bass

```python
import numpy as np
import jax
import jax.numpy as jnp

def _softmax(x, axis=-1):
    return jax.nn.softmax(x, axis=axis)

def _gelu(x):
    return jax.nn.gelu(x, approximate=True)

def _silu(x):
    return jax.nn.silu(x)

def _sigmoid(x):
    return jax.nn.sigmoid(x)

def _layernorm(x, axis=-1, eps=1e-05):
    m = jnp.mean(x, axis=axis, keepdims=True)
    v = jnp.var(x, axis=axis, keepdims=True)
    return (x - m) / jnp.sqrt(v + eps)

def _scatter_add(tgt, idx, src, axis=0):
    return tgt.at[idx].add(src)

def _segment_sum(src, seg, n):
    return jax.ops.segment_sum(src, seg, n)
kernel_name = 'mk_seq_postln_d1_jaxref_r4_5dff55'

def setup_inputs(seed: int=0):
    np.random.seed(seed)
    _w = jnp.asarray

    def _L0_attn_setup():
        import jax, jax.numpy as jnp
        import numpy as np
        B, S, D, H = (2, 512, 256, 16)
        HEAD_DIM = D // H
        WINDOW = 64
        DILATION = 1
        NEG = jnp.float32(-1000000000.0)

        def _build_attn_mask(seq_len):
            idx = jnp.arange(seq_len)
            diff = idx[None, :] - idx[:, None]
            mask = jnp.where(diff > 0, -jnp.inf, 0.0).astype(jnp.float32)
            cond = (jnp.abs(diff) <= WINDOW) & (jnp.abs(diff) % DILATION == 0)
            allowed = jnp.where(cond, 0.0, -jnp.inf).astype(jnp.float32)
            mask = jnp.maximum(mask, allowed)
            return jnp.maximum(mask, NEG)
        key = jax.random.key(seed)
        k = jax.random.split(key, 5)
        return {'x': jax.random.normal(k[0], (B, S, D), dtype=jnp.float32), 'in_proj_w': jax.random.normal(k[1], (3 * D, D), dtype=jnp.float32) * D ** (-0.5), 'in_proj_b': jax.random.normal(k[2], (3 * D,), dtype=jnp.float32) * 0.02, 'out_proj_w': jax.random.normal(k[3], (D, D), dtype=jnp.float32) * D ** (-0.5), 'out_proj_b': jax.random.normal(k[4], (D,), dtype=jnp.float32) * 0.02}
    _L0_attn_in = _L0_attn_setup()

    def _L0_ffn_setup():
        import jax, jax.numpy as jnp
        import numpy as np
        B, S, H = (1, 512, 256)
        E, K = (16, 4)
        G, TG = (4, 2)
        I_MOE = 128
        N_SH = 2
        SCALE = 2.5

        def _mlp(x, gw, uw, dw):
            return jax.nn.silu(x @ gw.T) * (x @ uw.T) @ dw.T

        def _route(x2d, router_weight, e_bias):
            T = x2d.shape[0]
            scores = jax.nn.sigmoid(x2d @ router_weight.T)
            sc = scores + e_bias[None, :]
            group_scores = jnp.sum(jax.lax.top_k(sc.reshape(T, G, E // G), 2)[0], axis=-1)
            _, gidx = jax.lax.top_k(group_scores, TG)
            gmask = jnp.zeros((T, G), sc.dtype).at[jnp.arange(T)[:, None], gidx].set(1.0)
            smask = jnp.repeat(gmask, E // G, axis=1)
            masked = jnp.where(smask > 0, sc, 0.0)
            _, tidx = jax.lax.top_k(masked, K)
            tw = jnp.take_along_axis(scores, tidx, axis=1)
            tw = tw / (jnp.sum(tw, axis=-1, keepdims=True) + 1e-20)
            tw = tw * SCALE
            return (tidx, tw)

        def _moe_forward(hidden_states, router_weight, e_bias, gate_w, up_w, down_w, sh_gate_w, sh_up_w, sh_down_w):
            orig_shape = hidden_states.shape
            x = hidden_states.reshape(-1, H)
            T = x.shape[0]
            tidx, tw = _route(x, router_weight, e_bias)
            g = jnp.einsum('th,eih->tei', x, gate_w)
            u = jnp.einsum('th,eih->tei', x, up_w)
            h = jax.nn.silu(g) * u
            yo = jnp.einsum('tei,ehi->teh', h, down_w)
            combine = jnp.zeros((T, E), tw.dtype).at[jnp.arange(T)[:, None], tidx].add(tw)
            routed = jnp.einsum('te,teh->th', combine, yo)
            shared = _mlp(hidden_states.reshape(-1, H), sh_gate_w, sh_up_w, sh_down_w)
            return (routed + shared).reshape(orig_shape)
        key = jax.random.key(seed)
        ks = jax.random.split(key, 9)
        s = 0.02
        return {'hidden_states': jax.random.normal(ks[0], (B, S, H), jnp.float32), 'router_weight': jax.random.normal(ks[1], (E, H), jnp.float32) * s, 'e_bias': jnp.zeros((E,), jnp.float32), 'gate_w': jax.random.normal(ks[2], (E, I_MOE, H), jnp.float32) * s, 'up_w': jax.random.normal(ks[3], (E, I_MOE, H), jnp.float32) * s, 'down_w': jax.random.normal(ks[4], (E, H, I_MOE), jnp.float32) * s, 'sh_gate_w': jax.random.normal(ks[5], (N_SH * I_MOE, H), jnp.float32) * s, 'sh_up_w': jax.random.normal(ks[6], (N_SH * I_MOE, H), jnp.float32) * s, 'sh_down_w': jax.random.normal(ks[7], (H, N_SH * I_MOE), jnp.float32) * s}
    _L0_ffn_in = _L0_ffn_setup()
    _d = {'L0_attn_x': _L0_attn_in['x'], 'L0_attn_in_proj_w': _L0_attn_in['in_proj_w'], 'L0_attn_in_proj_b': _L0_attn_in['in_proj_b'], 'L0_attn_out_proj_w': _L0_attn_in['out_proj_w'], 'L0_attn_out_proj_b': _L0_attn_in['out_proj_b'], 'L0_ffn_router_weight': _L0_ffn_in['router_weight'], 'L0_ffn_e_bias': _L0_ffn_in['e_bias'], 'L0_ffn_gate_w': _L0_ffn_in['gate_w'], 'L0_ffn_up_w': _L0_ffn_in['up_w'], 'L0_ffn_down_w': _L0_ffn_in['down_w'], 'L0_ffn_sh_gate_w': _L0_ffn_in['sh_gate_w'], 'L0_ffn_sh_up_w': _L0_ffn_in['sh_up_w'], 'L0_ffn_sh_down_w': _L0_ffn_in['sh_down_w']}
    _x0 = _d['L0_attn_x']
    _d['L0_attn_x'] = jax.random.normal(jax.random.fold_in(jax.random.key(seed), 1), (4, 1024, 256), dtype=_x0.dtype)
    del _x0
    return _d

def reference(L0_attn_x, L0_attn_in_proj_w, L0_attn_in_proj_b, L0_attn_out_proj_w, L0_attn_out_proj_b, L0_ffn_router_weight, L0_ffn_e_bias, L0_ffn_gate_w, L0_ffn_up_w, L0_ffn_down_w, L0_ffn_sh_gate_w, L0_ffn_sh_up_w, L0_ffn_sh_down_w):

    def _L0_attn_ref(x, in_proj_w, in_proj_b, out_proj_w, out_proj_b):
        import jax, jax.numpy as jnp
        import numpy as np
        B, S, D, H = (2, 512, 256, 16)
        HEAD_DIM = D // H
        WINDOW = 64
        DILATION = 1
        NEG = jnp.float32(-1000000000.0)

        def _build_attn_mask(seq_len):
            idx = jnp.arange(seq_len)
            diff = idx[None, :] - idx[:, None]
            mask = jnp.where(diff > 0, -jnp.inf, 0.0).astype(jnp.float32)
            cond = (jnp.abs(diff) <= WINDOW) & (jnp.abs(diff) % DILATION == 0)
            allowed = jnp.where(cond, 0.0, -jnp.inf).astype(jnp.float32)
            mask = jnp.maximum(mask, allowed)
            return jnp.maximum(mask, NEG)
        b, s, d = x.shape
        qkv = x @ in_proj_w.T + in_proj_b
        q, k, v = jnp.split(qkv, 3, axis=-1)

        def to_heads(t):
            return t.reshape(b, s, H, HEAD_DIM).transpose(0, 2, 1, 3)
        q, k, v = (to_heads(q), to_heads(k), to_heads(v))
        scale = jnp.float32(HEAD_DIM) ** (-0.5)
        scores = jnp.einsum('bhqd,bhkd->bhqk', q * scale, k)
        mask = _build_attn_mask(s)
        scores = scores + mask[None, None, :, :]
        attn = jax.nn.softmax(scores, axis=-1)
        out = jnp.einsum('bhqk,bhkd->bhqd', attn, v)
        out = out.transpose(0, 2, 1, 3).reshape(b, s, d)
        return out @ out_proj_w.T + out_proj_b

    def _L0_ffn_ref(hidden_states, router_weight, e_bias, gate_w, up_w, down_w, sh_gate_w, sh_up_w, sh_down_w):
        import jax, jax.numpy as jnp
        import numpy as np
        B, S, H = (1, 512, 256)
        E, K = (16, 4)
        G, TG = (4, 2)
        I_MOE = 128
        N_SH = 2
        SCALE = 2.5

        def _mlp(x, gw, uw, dw):
            return jax.nn.silu(x @ gw.T) * (x @ uw.T) @ dw.T

        def _route(x2d, router_weight, e_bias):
            T = x2d.shape[0]
            scores = jax.nn.sigmoid(x2d @ router_weight.T)
            sc = scores + e_bias[None, :]
            group_scores = jnp.sum(jax.lax.top_k(sc.reshape(T, G, E // G), 2)[0], axis=-1)
            _, gidx = jax.lax.top_k(group_scores, TG)
            gmask = jnp.zeros((T, G), sc.dtype).at[jnp.arange(T)[:, None], gidx].set(1.0)
            smask = jnp.repeat(gmask, E // G, axis=1)
            masked = jnp.where(smask > 0, sc, 0.0)
            _, tidx = jax.lax.top_k(masked, K)
            tw = jnp.take_along_axis(scores, tidx, axis=1)
            tw = tw / (jnp.sum(tw, axis=-1, keepdims=True) + 1e-20)
            tw = tw * SCALE
            return (tidx, tw)

        def _moe_forward(hidden_states, router_weight, e_bias, gate_w, up_w, down_w, sh_gate_w, sh_up_w, sh_down_w):
            orig_shape = hidden_states.shape
            x = hidden_states.reshape(-1, H)
            T = x.shape[0]
            tidx, tw = _route(x, router_weight, e_bias)
            g = jnp.einsum('th,eih->tei', x, gate_w)
            u = jnp.einsum('th,eih->tei', x, up_w)
            h = jax.nn.silu(g) * u
            yo = jnp.einsum('tei,ehi->teh', h, down_w)
            combine = jnp.zeros((T, E), tw.dtype).at[jnp.arange(T)[:, None], tidx].add(tw)
            routed = jnp.einsum('te,teh->th', combine, yo)
            shared = _mlp(hidden_states.reshape(-1, H), sh_gate_w, sh_up_w, sh_down_w)
            return (routed + shared).reshape(orig_shape)
        return _moe_forward(hidden_states, router_weight, e_bias, gate_w, up_w, down_w, sh_gate_w, sh_up_w, sh_down_w)
    x = L0_attn_x
    x = _layernorm(x + _L0_attn_ref(x, L0_attn_in_proj_w, L0_attn_in_proj_b, L0_attn_out_proj_w, L0_attn_out_proj_b), axis=-1)
    x = _layernorm(x + _L0_ffn_ref(x, L0_ffn_router_weight, L0_ffn_e_bias, L0_ffn_gate_w, L0_ffn_up_w, L0_ffn_down_w, L0_ffn_sh_gate_w, L0_ffn_sh_up_w, L0_ffn_sh_down_w), axis=-1)
    return x

_drawn_inputs = setup_inputs


def setup_inputs(seed=0):
    import zlib

    import numpy as np

    out = dict(_drawn_inputs(seed))
    spreads = {'L0_ffn_e_bias': (0.0, 0.485)}
    factors = {'L0_attn_out_proj_b': 2.975,
     'L0_ffn_router_weight': 7.661,
     'L0_ffn_gate_w': 3.81,
     'L0_ffn_up_w': 3.765,
     'L0_ffn_down_w': 3.778,
     'L0_ffn_sh_gate_w': 3.392,
     'L0_ffn_sh_up_w': 3.359,
     'L0_ffn_sh_down_w': 3.36}
    for name, (base, spread) in spreads.items():
        noise = np.random.default_rng([zlib.crc32(name.encode()), seed]).standard_normal(out[name].shape)
        drawn = base * np.exp(spread * noise) if base else spread * noise
        out[name] = jnp.asarray(drawn.astype(out[name].dtype))
    for name, factor in factors.items():
        out[name] = (out[name] * factor).astype(out[name].dtype)
    return out
```

```python
import concourse.bass as bass
from concourse import mybir
from contextlib import ExitStack

F32 = mybir.dt.float32
F16 = mybir.dt.float16
ALU = mybir.AluOpType
ACT = mybir.ActivationFunctionType
AX = mybir.AxisListType

P = 128
B, S, D = 4, 1024, 256
T = B * S
H, HD = 16, 16
WIN = 64
NE, I, NSH, TOPK = 16, 128, 2, 4
NX = NE + NSH
EPS = 1e-5
CH = 512
NC = T // CH
NT = CH // P
KD = D // P
NH2 = S // CH
WSC = 64.0
BIG = 32768.0

HG = 4
NG = H // HG
NR = B * NG
VW = HG * (HD + 1)
MR = 112
SLOTS = [(qc, kt, max(qc * CH, kt * P - WIN)) for qc in range(NH2) for kt in range(S // P)
         if kt * P - WIN < (qc + 1) * CH]
NSL = len(SLOTS)


def max_units():
    units = []
    for t in range(S // P):
        w = min(P * t + P + WIN, S)
        for piece, (lo, hi) in enumerate([(0, min(w, CH)), (CH, w)]):
            if hi > lo:
                n = {1: 1, 2: 2, 3: 2}.get(CH // (hi - lo), HG)
                units += [(t, piece, lo, hi, range(h, h + n)) for h in range(0, HG, n)]
    return units


UNITS = max_units()
NU = len(UNITS)
NEEDS = [0, next(u for u, (t, _, _, hi, _) in enumerate(UNITS) if t * P >= CH or hi > CH)]


SECOND = next(u for u, (t, *_) in enumerate(UNITS) if t * P >= CH)
TAIL = 5


def share(slot):
    cols = [(qc + 1) * CH - q0 for qc, _, q0 in SLOTS]
    lo, hi = (NU * sum(cols[:n]) // sum(cols) for n in (slot, slot + 1))
    return [((n - TAIL) % NU, n >= TAIL) for n in range(lo, hi)]


def settle(eng, sem):
    eng.sem_inc(sem, 1)


def wait(eng, sem, value):
    if not (isinstance(value, int) and value <= 0):
        eng.wait_ge(sem, value)


def rounds(eng, n, body):
    body(0, 0, 0)
    body(1, 1, 0)
    with eng.Fori(1, n // 2 - 1) as i:
        body(i * 2, 0, i)
        body(i * 2 + 1, 1, i)
    body(n - 2, 0, n // 2 - 1)
    body(n - 1, 1, n // 2 - 1, last=True)


def attention_moe(nc, x, xT, winT, bqkT, bvr, woutT, bout, rwT, ebias, gwT, uwT, dwT, sgT, suT, sdT, out):
    with ExitStack() as ctx:
        q_dram = nc.dram_tensor("q_dram", [2, B * D // 2, NH2, 2, CH], F16).ap()
        k_dram = nc.dram_tensor("k_dram", [2, B * D // 2, NH2, 2, CH], F16).ap()
        c_dram = nc.dram_tensor("c_dram", [NE, T], F32).ap()
        banks = [ctx.enter_context(nc.psum_tensor(f"bank{i}", [P, CH], F32)) for i in range(8)]

        def keep(name, shape, dt):
            return ctx.enter_context(nc.sbuf_tensor(name, shape, dt))

        def opener(where, prefix):
            def sb(name, shape, dt):
                return where.enter_context(nc.sbuf_tensor(prefix + name, shape, dt))

            def sems(names):
                return {n: where.enter_context(nc.semaphore(prefix + n)) for n in names.split()}
            return sb, sems

        ident = keep("ident", [P, P], F32)
        o_all = keep("o_all", [P, NH2, NR, NT, HG * HD], F32)
        wh = {"g": keep("gh", [P, KD, NX, I], F16), "u": keep("uh", [P, KD, NX, I], F16), "d": keep("dh", [P, NX, D], F16)}
        wl = {"g": keep("gl", [P, KD, NX, I], F16), "u": keep("ul", [P, KD, NX, I], F16), "d": keep("dl", [P, NX, D], F16)}

        with ExitStack() as att:
            v_all = att.enter_context(nc.sbuf_tensor("v_all", [P, NR, S // P, VW], F32))
            with ExitStack() as st:
                projection(nc, *opener(st, "p_"), banks, ident, v_all, q_dram, k_dram, xT, winT, bqkT, bvr)
            with ExitStack() as st:
                attention(nc, *opener(st, "a_"), banks, ident, v_all, o_all, wh, wl, q_dram, k_dram,
                          gwT, uwT, dwT, sgT, suT, sdT)
        with ExitStack() as st:
            experts(nc, *opener(st, "e_"), banks, ident, o_all, wh, wl, c_dram, x, woutT, bout, rwT, ebias, out)


def projection(nc, sb, sems, banks, ident, v_all, q_dram, k_dram, xT, winT, bqkT, bvr):
    stage = sb("stage", [P, KD, 3 * D], F32)
    winh = sb("winh", [P, KD, 3 * D], F16)
    winl = sb("winl", [P, KD, 3 * D], F16)
    bqk = sb("bqk", [P, 4], F32)
    bqs = sb("bqs", [P, 4], F32)
    bv = sb("bv", [P, NG, HG * HD], F32)
    xf = [sb(f"xf{p}", [P, KD, CH], F32) for p in range(2)]
    xh = [sb(f"xh{p}", [P, KD, CH], F16) for p in range(2)]
    xl = [sb(f"xl{p}", [P, KD, CH], F16) for p in range(2)]
    qkf = [sb(f"qkf{m}", [P, CH], F32) for m in range(4)]
    qk16 = [sb(f"qk16{p}", [P, 2, 4, CH], F16) for p in range(2)]
    s = sems("""w_loaded b_loaded w_hi w_lo bias_done ident_zero ident_done ones_done x_loaded0 x_loaded1 x_hi
        x_split proj_ready qk_f32 qk_hi qk_lo v_done qk_written0 qk_written1 settled""")
    x_loaded = [s["x_loaded0"], s["x_loaded1"]]
    qk_written = [s["qk_written0"], s["qk_written1"]]
    NM = 6

    with nc.Block() as block:

        @block.sync
        def _(sp):
            def load_x(c, p):
                sp.dma_start(xf[p][:], xT[:, bass.ds(c * CH, CH)].rearrange("(k p) t -> p k t", p=P))\
                  .then_inc(x_loaded[p], 16)

            load_x(0, 0)
            for k in range(KD):
                sp.dma_start(stage[:, k, :], winT.rearrange("(k p) n -> p k n", p=P)[:, k]).then_inc(s["w_loaded"], 16)
            sp.dma_start(bqk[:], bqkT).then_inc(s["b_loaded"], 16)
            sp.dma_start(bv[:].rearrange("p g n -> p (g n)"), bvr.partition_broadcast(P)).then_inc(s["b_loaded"], 16)
            load_x(1, 1)

            def body(c, p, k, last=False):
                if not (isinstance(c, int) and c >= NC - 2):
                    sp.wait_ge(s["x_split"], c + 1)
                    load_x(c + 2, p)
                sp.wait_ge(s["qk_lo"], c * 4 + 4)
                settle(sp, s["settled"])
                for part in range(2):
                    for m in range(4):
                        dst = (q_dram, k_dram)[m // 2][part, bass.ds(k * (D // 2) + (m % 2) * HD * HG, HD * HG), p]
                        sp.dma_start(dst, qk16[p][:, part, m, :])\
                          .then_inc(qk_written[p], 16)
            rounds(sp, NC, body)
            for p in range(2):
                sp.wait_ge(qk_written[p], 128 * (NC // 2))

        @block.gpsimd
        def _(pool):
            pool.memset(ident[:], 0.0).then_inc(s["ident_zero"], 1)
            pool.memset(v_all[:, :, :, HG * HD:VW], 1.0).then_inc(s["ones_done"], 1)
            pool.wait_ge(s["ident_zero"], 1)
            pool.affine_select(out=ident[:], in_=ident[:], compare_op=ALU.not_equal, fill=1.0, base=0,
                               pattern=[[-1, P]], channel_multiplier=1).then_inc(s["ident_done"], 1)

            def split_x(c, p):
                pool.wait_ge(s["x_hi"], c + 1)
                settle(pool, s["settled"])
                pool.tensor_tensor(xl[p][:], xf[p][:], xh[p][:], op=ALU.subtract).then_inc(s["x_split"], 1)

            def body(c, p, k, last=False):
                if not last:
                    split_x(c + 1, 1 - p)
                for m in range(4):
                    pool.wait_ge(s["qk_hi"], c * 4 + m + 1)
                    pool.tensor_tensor(qk16[p][:, 1, m, :], qkf[m][:], qk16[p][:, 0, m, :], op=ALU.subtract)\
                        .then_inc(s["qk_lo"], 1)

            split_x(0, 0)
            rounds(pool, NC, body)

        @block.tensor
        def _(pe):
            pe.wait_ge(s["w_lo"], 1)

            def body(c, p, k, last=False):
                pe.wait_ge(s["x_split"], c + 1)
                for m in range(NM):
                    bank = banks[m]
                    if m < 4:
                        wait(pe, s["qk_f32"], c * 4 - 4 + m + 1)
                    else:
                        wait(pe, s["v_done"], c * NT - NT + 2 * (m - 3))
                    for half in range(1 if m < 4 else 2):
                        n = 0
                        for w, xx in ((winh, xh[p]), (winh, xl[p]), (winl, xh[p])):
                            for kk in range(KD):
                                if m < 4:
                                    mm = pe.matmul(bank[:], w[:, kk, m * P:m * P + P], xx[:, kk, :],
                                                   start=(n == 0), stop=(n == 5))
                                else:
                                    lo = (2 * (m - 4) + half) * P
                                    mm = pe.matmul(bank[:, half * D:half * D + D], xx[:, kk, lo:lo + P],
                                                   w[:, kk, 2 * D:3 * D], start=(n == 0), stop=(n == 5))
                                n += 1
                    mm.then_inc(s["proj_ready"], 1)

            rounds(pe, NC, body)

        @block.scalar
        def _(act):
            def hi_x(c, p, k):
                act.wait_ge(x_loaded[p], k * 16 + 16)
                wait(act, s["proj_ready"], (c - 1) * NM)
                act.copy(xh[p][:], xf[p][:]).then_inc(s["x_hi"], 1)

            act.wait_ge(s["w_loaded"], 16 * KD)
            act.mul(winh[:], stage[:], WSC).then_inc(s["w_hi"], 1)
            hi_x(0, 0, 0)
            act.wait_ge(s["b_loaded"], 32)
            act.mul(bqs[:, 0:2], bqk[:, 0:2], HD ** -0.5).then_inc(s["bias_done"], 1)
            act.copy(bqs[:, 2:4], bqk[:, 2:4]).then_inc(s["bias_done"], 1)
            act.wait_ge(s["bias_done"], 2)

            def body(c, p, k, last=False):
                if not last:
                    hi_x(c + 1, 1 - p, k + p)
                for m in range(4):
                    act.wait_ge(s["proj_ready"], c * NM + m + 1)
                    wait(act, s["qk_lo"], c * 4 - 4 + m + 1)
                    scale = (HD ** -0.5 if m < 2 else 1.0) / WSC
                    act.activation(qkf[m][:], banks[m][:], ACT.Identity, bias=bqs[:, m:m + 1], scale=scale)\
                       .then_inc(s["qk_f32"], 1)

            rounds(act, NC, body)

        @block.vector
        def _(dve):
            dve.wait_ge(s["w_hi"], 1)
            dve.scalar_tensor_tensor(winl[:], stage[:], WSC, winh[:], op0=ALU.mult, op1=ALU.subtract)\
               .then_inc(s["w_lo"], 1)
            dve.wait_ge(s["b_loaded"], 32)

            def body(c, p, k, last=False):
                for m in range(4):
                    dve.wait_ge(s["qk_f32"], c * 4 + m + 1)
                    if m == 0:
                        wait(dve, qk_written[p], k * 128)
                    dve.tensor_copy(qk16[p][:, 0, m, :], qkf[m][:]).then_inc(s["qk_hi"], 1)
                for j in range(NT):
                    dve.wait_ge(s["proj_ready"], c * NM + 5 + j // 2)
                    dve.scalar_tensor_tensor(v_all[:, bass.ds(k * NG, NG), p * NT + j, 0:HG * HD],
                                             banks[4 + j // 2][:, (j % 2) * D:(j % 2) * D + D]
                                             .rearrange("p (g n) -> p g n", g=NG), 1.0 / WSC, bv[:],
                                             op0=ALU.mult, op1=ALU.add).then_inc(s["v_done"], 1)

            rounds(dve, NC, body)


def attention(nc, sb, sems, banks, ident, v_all, o_all, wh, wl, q_dram, k_dram, gwT, uwT, dwT, sgT, suT, sdT):
    QS = [sb(f"QS{p}", [P, NH2, HG, CH], F16) for p in range(2)]
    KS = [sb(f"KS{p}", [P, NH2, HG // 2, CH], F16) for p in range(2)]
    VG = [sb(f"VG{p}", [P, S // P, VW], F32) for p in range(2)]
    PT = [[sb(f"PT{p}{h}", [P, CH], F32) for h in range(HG)] for p in range(2)]
    idb = sb("idb", [P, P], F16)
    tri = sb("tri", [P, P], F16)
    triT = sb("triT", [P, P], F16)
    mx = sb("mx", [P, 2, NH2, HG, NT], F32)
    mT = [sb(f"mT{half}", [HG * NT, P], F16) for half in range(NH2)]
    OTs = sb("OTs", [P, CH], F32)
    rec = sb("rec", [P, NT, HG], F32)
    raw = [sb(f"raw{p}", [P, 2 * KD * I + D], F32) for p in range(2)]
    s = sems("""zeroed stack_zero tri_done stack_const otb_zero stacked00 stacked01 stacked10 stacked11 negmax00 negmax01 negmax10 negmax11 v_copied s_ready
        max_done both_max mT_ready mT_done st_ready exp_done pv_done ot_done ott_ready rec_done o_done
        raw_loaded0 raw_loaded1 w_hi w_lo settled""")
    stacked = [[s[f"stacked{half}{p}"] for p in range(2)] for half in range(NH2)]
    negmax = [[s[f"negmax{half}{p}"] for p in range(2)] for half in range(NH2)]
    raw_loaded = [s["raw_loaded0"], s["raw_loaded1"]]
    sbank, stbank, otbank, aux = banks[0:3], banks[3:6], banks[6], banks[7]
    NRAW = 2 * KD + 1
    NST = NSL * HG
    LAST_OF = [max(u for u in range(NST) if u % 3 == n) for n in range(3)]
    HALF = [max(i for i, sl in enumerate(SLOTS) if sl[0] == qc) for qc in range(NH2)]
    FIRST = 1 + max(i for i, (qc, kt, _) in enumerate(SLOTS) if qc == 0 or kt < CH // P)
    MAXT, OTT = [FIRST, 1], [HALF[0] + 3, 2]

    def parts(w):
        return (w[:, 0:KD * I].rearrange("p (k i) -> p k i", k=KD),
                w[:, KD * I:2 * KD * I].rearrange("p (k i) -> p k i", k=KD), w[:, 2 * KD * I:])

    def split_of(w, n):
        return (w["g"][:, :, bass.ds(n, 1), :].squeeze(2), w["u"][:, :, bass.ds(n, 1), :].squeeze(2),
                w["d"][:, bass.ds(n, 1), :].squeeze(1))

    with nc.Block() as block:

        @block.sync
        def _(sp):
            def stack(G, p, half):
                for e in range(2):
                    for dst, src, n, both_at, one_at in ((QS[p], q_dram, HG // 2, 0, 2 * HD), (KS[p], k_dram, 0, HD, 0)):
                        a = src[:, bass.ds(G * (2 * HD) + e * HD, HD), half].rearrange("s d i t -> s d (i t)")
                        to = dst[:, half, n * e:n * e + 2, :].rearrange("p i t -> p (i t)")
                        at = 64 * e + both_at
                        sp.dma_start(to[at:at + 2 * HD], a).then_inc(stacked[half][p], 16)
                        at = 64 * e + one_at
                        sp.dma_start(to[at:at + HD], a[0]).then_inc(stacked[half][p], 16)

            def load_raw(n, p):
                wait(sp, s["w_lo"], (n - 1) * 3)
                g, u, d = parts(raw[p])
                if isinstance(n, int) and n < NSH:
                    gs, us = (a.rearrange("(k p) (e i) -> k p e i", p=P, i=I)[:, :, n, :] for a in (sgT, suT))
                    src = sdT.rearrange("(e i) n -> e i n", i=I)[n]
                else:
                    gs, us = (a[:, bass.ds(n - NSH, 1), :].squeeze(1).rearrange("(k p) i -> k p i", p=P)
                              for a in (gwT, uwT))
                    src = dwT[:, bass.ds(n - NSH, 1), :].squeeze(1)
                for kk in range(KD):
                    sp.dma_start(g[:, kk, :], gs[kk]).then_inc(raw_loaded[p], 16)
                    sp.dma_start(u[:, kk, :], us[kk]).then_inc(raw_loaded[p], 16)
                sp.dma_start(d, src).then_inc(raw_loaded[p], 16)

            def put_max(G, p, half):
                sp.wait_ge(s["mT_done"], G * NH2 + half + 1)
                sp.dma_start(QS[p][MR:MR + 1, half, :, :].rearrange("o h t -> o (h t)"), mT[half][:])\
                  .then_inc(negmax[half][p], 16)

            sp.wait_ge(s["stack_const"], 4)
            for G in range(2):
                for half in range(NH2):
                    stack(G, G, half)
            for n in range(NSH):
                load_raw(n, n)
            put_max(0, 0, 0)

            def body(G, p, k, last=False):
                more = not (isinstance(G, int) and G >= NR - 2)
                put_max(G, p, 1)
                load_raw(G + NSH, p)
                if more:
                    sp.wait_ge(s["st_ready"], G * NST + FIRST * HG)
                    stack(G + 2, p, 0)
                if not last:
                    put_max(G + 1, 1 - p, 0)
                if more:
                    sp.wait_ge(s["st_ready"], G * NST + NST)
                    stack(G + 2, p, 1)

            rounds(sp, NR, body)

        @block.gpsimd
        def _(pool):
            pool.memset(idb[:], 0.0).then_inc(s["zeroed"], 1)
            pool.memset(tri[:], 0.0).then_inc(s["zeroed"], 1)
            pool.memset(triT[:], 0.0).then_inc(s["zeroed"], 1)
            pool.wait_ge(s["zeroed"], 3)
            pool.affine_select(out=idb[:], in_=idb[:], compare_op=ALU.not_equal, fill=BIG, base=0,
                               pattern=[[-1, P]], channel_multiplier=1).then_inc(s["tri_done"], 1)
            pool.affine_select(out=tri[:], in_=tri[:], compare_op=ALU.is_ge, fill=-BIG, base=0,
                               pattern=[[-1, P]], channel_multiplier=1).then_inc(s["tri_done"], 1)
            pool.affine_select(out=triT[:], in_=triT[:], compare_op=ALU.is_ge, fill=-BIG, base=0,
                               pattern=[[1, P]], channel_multiplier=-1).then_inc(s["tri_done"], 1)

            def copy_v(G, p):
                wait(pool, s["pv_done"], (G - 1) * NSL)
                settle(pool, s["settled"])
                pool.tensor_copy(VG[p][:], v_all[:, bass.ds(G, 1), :, :].squeeze(1)).then_inc(s["v_copied"], 1)

            def body(G, p, k, last=False):
                if not last:
                    copy_v(G + 1, 1 - p)

            copy_v(0, 0)
            rounds(pool, NR, body)

        @block.tensor
        def _(pe):
            def scores(G, p, k, u):
                t, piece, lo, hi, heads = UNITS[u]
                bank = sbank[u % 3]
                for half in range(NH2):
                    if u == NEEDS[half]:
                        pe.wait_ge(stacked[half][p], k * 128 + 128)
                wait(pe, s["max_done"], G * NU + u - 2)
                for n, h in enumerate(heads):
                    at = n * (hi - lo)
                    m0, m1 = max(lo, P * t + WIN), hi
                    mm = pe.matmul(bank[:, at:at + hi - lo], QS[p][0:MR, t // NT, h, t % NT * P:t % NT * P + P],
                                   KS[p][0:MR, piece, h % 2, 0:hi - lo], start=True, stop=(m1 <= m0))
                    if m1 > m0:
                        mm = pe.matmul(bank[:, at + m0 - lo:at + hi - lo], idb[:],
                                       tri[:, m0 - P * t - WIN:m1 - P * t - WIN], start=False, stop=True)
                mm.then_inc(s["s_ready"], 1)

            def scoresT(G, p, k, i, h):
                qc, kt, q0 = SLOTS[i]
                u = i * HG + h
                if kt == 0 and h == 0:
                    pe.wait_ge(negmax[qc][p], k * 16 + 16)
                wait(pe, s["exp_done"], G * NST + (u - 2 if u >= 3 else LAST_OF[u] - NST + 1))
                q1 = (qc + 1) * CH
                m0, m1 = q0, min(q1, kt * P + WIN)
                bank = stbank[u % 3]
                mm = pe.matmul(bank[:, 0:q1 - q0], KS[p][0:MR + 1, kt // NT, h % 2, kt % NT * P:kt % NT * P + P],
                               QS[p][0:MR + 1, qc, h, q0 - qc * CH:CH], start=True, stop=(m1 <= m0))
                if m1 > m0:
                    at = m0 - (kt * P - WIN)
                    mm = pe.matmul(bank[:, 0:m1 - m0], idb[:], triT[:, at:at + m1 - m0], start=False, stop=True)
                mm.then_inc(s["st_ready"], 1)

            def weighted(G, p, i):
                qc, kt, q0 = SLOTS[i]
                if i == 0:
                    pe.wait_ge(s["v_copied"], G + 1)
                if kt == 0:
                    wait(pe, s["ot_done"], G * NH2 + qc)
                pe.wait_ge(s["exp_done"], G * NST + (i + 1) * HG)
                for h in range(HG):
                    mm = pe.matmul(otbank[32 * h:32 * h + HD + 1, q0 - qc * CH:CH], VG[p][:, kt, h:VW:HG],
                                   PT[(p + i) % 2][h][:, 0:(qc + 1) * CH - q0], start=(kt == 0),
                                   stop=(i in HALF), skip_group_check=True)
                mm.then_inc(s["pv_done"], 1)

            def maxT(G, half):
                pe.wait_ge(s["both_max"], G * NH2 + half + 1)
                if half:
                    pe.wait_ge(s["mT_done"], G * NH2 + 1)
                else:
                    wait(pe, s["o_done"], NH2 * G - 1)
                pe.transpose(aux[0:HG * NT, 0:P], mx[:, 0, half].rearrange("p h t -> p (h t)"), ident[:])\
                  .then_inc(s["mT_ready"], 1)

            def outT(G, qc):
                pe.wait_ge(s["ot_done"], G * NH2 + qc + 1)
                if qc and not (isinstance(G, int) and G == NR - 1):
                    pe.wait_ge(s["mT_done"], (G + 1) * NH2 + NH2)
                else:
                    wait(pe, s["o_done"], G * NH2 + qc)
                for j in range(NT):
                    mm = pe.transpose(aux[:, j * P:j * P + P], OTs[:, j * P:j * P + P], ident[:])
                mm.then_inc(s["ott_ready"], 1)

            pe.wait_ge(s["tri_done"], 3)
            for u in range(NU - TAIL):
                scores(0, 0, 0, u)
            maxT(0, 0)
            pe.wait_ge(s["otb_zero"], 1)

            def body(G, p, k, last=False):
                def some_scores(units):
                    for u, ahead in units:
                        if not ahead:
                            scores(G, p, k, u)
                        elif not last:
                            scores(G + 1, 1 - p, k + p, u)

                for i in range(NSL):
                    rest = share(i)
                    for h in range(HG):
                        scoresT(G, p, k, i, h)
                        some_scores(rest[h:h + 1])
                    some_scores(rest[HG:])
                    if i:
                        weighted(G, p, i - 1)
                    if i == MAXT[1]:
                        maxT(G, 1)
                    if i == OTT[1] and not (isinstance(G, int) and G == 0):
                        outT(G - 1, 1)
                    if i == OTT[0]:
                        outT(G, 0)
                    if i == MAXT[0] and not last:
                        maxT(G + 1, 0)
                weighted(G, p, NSL - 1)

            rounds(pe, NR, body)
            outT(NR - 1, 1)

        @block.scalar
        def _(act):
            def split_hi(n, p, k):
                act.wait_ge(raw_loaded[p], (k + 1) * 16 * NRAW)
                for src, dst in zip(parts(raw[p]), split_of(wh, n)):
                    act.mul(dst, src, WSC).then_inc(s["w_hi"], 1)

            def exp(G, p, i, h):
                qc, kt, q0 = SLOTS[i]
                u = i * HG + h
                act.wait_ge(s["st_ready"], G * NST + u + 1)
                if h == 0:
                    wait(act, s["pv_done"], G * NSL + i - 1)
                w = (qc + 1) * CH - q0
                act.activation(PT[(p + i) % 2][h][:, 0:w], stbank[u % 3][:, 0:w], ACT.Exp).then_inc(s["exp_done"], 1)

            def out_copy(G, qc):
                act.wait_ge(s["pv_done"], G * NSL + HALF[qc] + 1)
                wait(act, s["ott_ready"], G * NH2 + qc)
                act.copy(OTs[:], otbank[:]).then_inc(s["ot_done"], 1)

            def mT_copy(G, p, k, half):
                act.wait_ge(s["mT_ready"], G * NH2 + half + 1)
                if not (isinstance(G, int) and G == 0):
                    act.wait_ge(negmax[half][1 - p], (k + p) * 16)
                act.mul(mT[half][:], aux[0:HG * NT, 0:P], -1.0).then_inc(s["mT_done"], 1)

            for n in range(NSH):
                split_hi(n, n, 0)
            mT_copy(0, 0, 0, 0)

            def body(G, p, k, last=False):
                for i in range(NSL):
                    for h in range(HG):
                        exp(G, p, i, h)
                    if i == 0 and not (isinstance(G, int) and G == 0):
                        out_copy(G - 1, NH2 - 1)
                    if i == HALF[0] + 1:
                        out_copy(G, 0)
                    if i == HALF[0]:
                        split_hi(G + NSH, p, k + 1)
                    if i == MAXT[1]:
                        mT_copy(G, p, k, 1)
                    if i == MAXT[0] and not last:
                        mT_copy(G + 1, 1 - p, k + p, 0)

            rounds(act, NR, body)
            out_copy(NR - 1, NH2 - 1)

        @block.vector
        def _(dve):
            for a in (*QS, *KS):
                last_ = dve.memset(a[:], 0.0)
            last_.then_inc(s["stack_zero"], 1)
            dve.wait_ge(s["stack_zero"], 1)
            for a in KS:
                dve.memset(a[96:P], 1.0).then_inc(s["stack_const"], 2)
            dve.memset(otbank[:], 0.0).then_inc(s["otb_zero"], 1)

            def smax(G, p, u):
                t, piece, lo, hi, heads = UNITS[u]
                n, w = len(heads), hi - lo
                dve.wait_ge(s["s_ready"], G * NU + u + 1)
                if u in (0, SECOND):
                    wait(dve, s["mT_ready"], G * NH2 - 1 + (u == SECOND))
                dve.tensor_reduce(mx[:, piece, t // NT, heads[0]:heads[0] + n, t % NT],
                                  sbank[u % 3][:, 0:n * w].rearrange("p (h k) -> p h k", h=n),
                                  AX.X, ALU.max).then_inc(s["max_done"], 1)

            def both(G, half):
                dve.wait_ge(s["max_done"], G * NU + (NU if half else SECOND))
                a, b = (mx[:, n, half, :, 0 if half else NT - 1:NT] for n in range(2))
                dve.tensor_tensor(a, a, b, op=ALU.max).then_inc(s["both_max"], 1)

            def normal(G, qc):
                n = G * NH2 + qc
                dve.wait_ge(s["ott_ready"], n + 1)
                o = aux[:].rearrange("p (j h e) -> p j h e", j=NT, e=32)
                dve.reciprocal(rec[:].unsqueeze(3), o[:, :, :, HD:HD + 1]).then_inc(s["rec_done"], 1)
                dve.wait_ge(s["rec_done"], n + 1)
                dst = o_all[:, qc, bass.ds(G, 1), :, :].squeeze(1)
                for j in range(NT):
                    mm = dve.tensor_tensor(dst[:, j, :].rearrange("p (h d) -> p h d", d=HD), o[:, j, :, 0:HD],
                                           rec[:, j, :].unsqueeze(2).to_broadcast([P, HG, HD]), op=ALU.mult)
                mm.then_inc(s["o_done"], 1)

            def split_lo(n, p):
                for i, (src, hi_, dst) in enumerate(zip(parts(raw[p]), split_of(wh, n), split_of(wl, n))):
                    dve.wait_ge(s["w_hi"], 3 * n + i + 1)
                    dve.scalar_tensor_tensor(dst, src, WSC, hi_, op0=ALU.mult, op1=ALU.subtract)\
                       .then_inc(s["w_lo"], 1)

            for u in range(NU - TAIL):
                smax(0, 0, u)
            both(0, 0)
            for n in range(NSH):
                split_lo(n, n)

            def body(G, p, k, last=False):
                for i in range(NSL):
                    for u, ahead in share(i):
                        if not ahead:
                            smax(G, p, u)
                        elif not last:
                            smax(G + 1, 1 - p, u)
                    if i == MAXT[1]:
                        both(G, 1)
                    if i == OTT[1] and not (isinstance(G, int) and G == 0):
                        normal(G - 1, 1)
                    if i == OTT[0]:
                        normal(G, 0)
                    if i == MAXT[0] - 1 and not last:
                        both(G + 1, 0)
                    if i == HALF[0] + 1:
                        split_lo(G + NSH, p)

            rounds(dve, NR, body)
            normal(NR - 1, NH2 - 1)


def experts(nc, sb, sems, banks, ident, o_all, wh, wl, c_dram, x, woutT, bout, rwT, ebias, out):
    G, U, Y, X = banks[0:2], banks[2:4], banks[4:6], banks[6:8]
    NCB, NHB = 4, 3
    wo = sb("wo", [P, KD, D], F32)
    rwf = sb("rwf", [P, KD, NE], F32)
    rwh = sb("rwh", [P, KD, NE], F16)
    rwl = sb("rwl", [P, KD, NE], F16)
    bo = sb("bo", [P, D], F32)
    eb = sb("eb", [P, NE], F32)
    x1h = sb("x1h", [P, KD, T], F16)
    x1l = sb("x1l", [P, KD, T], F16)
    On = sb("On", [P, NT, D], F32)
    OnT = sb("OnT", [P, KD, CH], F32)
    xb = sb("xb", [P, NT, D], F32)
    x1c = sb("x1c", [P, NT, D], F32)
    zz, st, mv, ve, rstd = ([sb(f"{n}{w}", [P, *shape], F32) for w in range(2)] for n, shape in
                            (("z", (NT, D)), ("st", (NT, 6)), ("mv", (NT, 2)), ("ve", (NT,)), ("rstd", (NT,))))
    mhalf = sb("mhalf", [P, NT], F32)
    th = sb("th", [P, NT, NE], F32)
    sc = sb("sc", [P, NT, NE], F32)
    vm = sb("vm", [P, NT, NE], F32)
    pr = [sb(f"pr{i}", [P, NT, 4], F32) for i in range(2)]
    rk = sb("rk", [P, NT, 4], F32)
    gt = sb("gt", [P, NT, NE, NE], F16)
    eq = sb("eq", [P, NT, NE, NE], F16)
    tri = sb("tri", [P, NE, NE], F16)
    rank = sb("rank", [P, NT, NE], F32)
    tot = sb("tot", [P, NT], F32)
    cw = sb("cw", [P, NT, NE], F32)
    cT = sb("cT", [NE, CH], F32)
    cb = [sb(f"cb{i}", [P, CH], F32) for i in range(NCB)]
    sg = [sb(f"sg{i}", [P, CH], F32) for i in range(2)]
    hf = [sb(f"hf{i}", [P, CH], F32) for i in range(2)]
    hh = [sb(f"hh{i}", [P, CH], F16) for i in range(NHB)]
    hl = [sb(f"hl{i}", [P, CH], F16) for i in range(NHB)]
    oo = sb("oo", [P, NT, D], F32)

    s = sems("""w_loaded consts rw_hi rw_lo on_copied ont_ready ont_done xb_loaded xb_done y_ready z_done
        stats_done var_done eps_done rstd_done x1_done x1t_ready x1_hi x1_lo x1_kept lg_ready th_done route_step
        c_done cT_ready cT_done cT_written g_ready u_ready silu_done sc_done h_done hi_done lo_done down_done
        z2_done stats2_done var2_done eps2_done rstd2_done out_ready out_written settled""")
    c_loaded = list(sems(" ".join(f"c_loaded{i}" for i in range(NCB))).values())
    LAG = 2

    def kept(c):
        return o_all[:].rearrange("p h (b g) j n -> p (h b) g j n", g=NG)[:, bass.ds(c, 1)].squeeze(1)

    def tiles(a):
        return a[:].rearrange("p j (g n) -> p g j n", g=NG)

    STEPS = {0: "on", 1: "ont", 3: "y", 4: "var", 6: "norm", 7: "x1t", 9: "logits", 10: "route0", 11: "route1",
             12: "route2", 13: "route3", 14: "route4", 16: "cT"}

    with nc.Block() as block:

        @block.sync
        def _(sp):
            sp.dma_start(wo[:], woutT.rearrange("(k p) n -> p k n", p=P)).then_inc(s["w_loaded"], 16)
            sp.dma_start(rwf[:], rwT.rearrange("(k p) n -> p k n", p=P)).then_inc(s["w_loaded"], 16)
            sp.dma_start(bo[:], bout.partition_broadcast(P)).then_inc(s["w_loaded"], 16)
            sp.dma_start(eb[:], ebias.partition_broadcast(P)).then_inc(s["w_loaded"], 16)

            def load_x(c):
                wait(sp, s["z_done"], c * 2)
                sp.dma_start(xb[:], x[bass.ds(c * CH, CH), :].rearrange("(j p) n -> p j n", p=P))\
                  .then_inc(s["xb_loaded"], 16)

            def store_c(c):
                sp.wait_ge(s["cT_done"], c + 1)
                sp.dma_start(c_dram[:, bass.ds(c * CH, CH)], cT[:]).then_inc(s["cT_written"], 16)

            def load_c(t, e):
                if e == 0:
                    sp.wait_ge(s["cT_written"], t * 16 + 16)
                    settle(sp, s["settled"])
                wait(sp, s["sc_done"], t * NE + e - NCB + 1)
                sp.dma_start(cb[e % NCB][:], c_dram[e, bass.ds(t * CH, CH)].partition_broadcast(P))\
                  .then_inc(c_loaded[e % NCB], 16)

            def body(t, first=False, last=False):
                for e in range(NE):
                    load_c(t, e)
                    if e == 8 and not first:
                        sp.wait_ge(s["out_ready"], t * NT)
                        sp.dma_start(out[bass.ds((t - 1) * CH, CH), :].rearrange("(j p) n -> p j n", p=P), oo[:])\
                          .then_inc(s["out_written"], 16)
                    if e == 4 and not last:
                        load_x2(t)
                    if e == NE - 1 and not last:
                        store_c(t + 1)

            def load_x2(t):
                if not (isinstance(t, int) and t >= NC - 2):
                    load_x(t + 2)

            load_x(0)
            load_x(1)
            store_c(0)
            body(0, first=True)
            with sp.Fori(1, NC - 2) as t:
                body(t)
            body(NC - 2)
            body(NC - 1, last=True)
            sp.wait_ge(s["out_ready"], NC * NT)
            sp.dma_start(out[(NC - 1) * CH:, :].rearrange("(j p) n -> p j n", p=P), oo[:]).then_inc(s["out_written"], 16)
            sp.wait_ge(s["out_written"], 16 * NC)

        @block.gpsimd
        def _(pool):
            pool.memset(mhalf[:], -0.5).then_inc(s["consts"], 1)
            pool.memset(tri[:], 1.0).then_inc(s["consts"], 1)
            pool.wait_ge(s["consts"], 2)
            pool.affine_select(out=tri[:], in_=tri[:], compare_op=ALU.is_gt, fill=0.0, base=0,
                               pattern=[[1, NE], [-1, NE]], channel_multiplier=0).then_inc(s["consts"], 1)
            pool.wait_ge(s["w_loaded"], 64)

            def add_bo(c):
                pool.wait_ge(s["xb_loaded"], c * 16 + 16)
                for j in range(NT):
                    last_ = pool.tensor_tensor(xb[:, j, :], xb[:, j, :], bo[:], op=ALU.add)
                last_.then_inc(s["xb_done"], 1)

            def rstd_(w, c, var, eps, done):
                pool.wait_ge(var, c * NT + NT)
                settle(pool, s["settled"])
                pool.tensor_scalar(ve[w][:], mv[w][:, :, 1], EPS, None, op0=ALU.add).then_inc(eps, 1)
                pool.wait_ge(eps, c + 1)
                pool.tensor_tensor(rstd[w][:], ve[w][:], mhalf[:], op=ALU.pow).then_inc(done, 1)

            def first_norm(c):
                rstd_(0, c, s["var_done"], s["eps_done"], s["rstd_done"])
                pool.wait_ge(s["x1_done"], c * NT + NT)
                settle(pool, s["settled"])
                pool.tensor_copy(kept(c), tiles(x1c)).then_inc(s["x1_kept"], 1)

            def second_norm(t):
                rstd_(1, t, s["var2_done"], s["eps2_done"], s["rstd2_done"])

            add_bo(0)
            first_norm(0)
            add_bo(1)
            first_norm(1)
            with pool.Fori(2, NC) as c:
                add_bo(c)
                second_norm(c - 2)
                first_norm(c)
            second_norm(NC - 2)
            second_norm(NC - 1)

        @block.tensor
        def _(pe):
            def step(c, what):
                if what == "ont":
                    pe.wait_ge(s["on_copied"], c + 1)
                    for k in range(KD):
                        wait(pe, s["x1_lo"], c * KD)
                        wait(pe, s["cT_done"], c)
                        for j in range(NT):
                            mm = pe.transpose(X[k][:, j * P:j * P + P], On[:, j, k * P:k * P + P], ident[:])
                        mm.then_inc(s["ont_ready"], 1)
                elif what == "y":
                    pe.wait_ge(s["ont_done"], c * KD + KD)
                    for j in range(NT):
                        for k in range(KD):
                            mm = pe.matmul(X[j // 2][:, (j % 2) * D:(j % 2) * D + D], OnT[:, k, j * P:j * P + P],
                                           wo[:, k, :], start=(k == 0), stop=(k == KD - 1))
                    mm.then_inc(s["y_ready"], 1)
                elif what == "x1t":
                    pe.wait_ge(s["x1_done"], c * NT + NT)
                    for k in range(KD):
                        for j in range(NT):
                            mm = pe.transpose(X[k][:, j * P:j * P + P], x1c[:, j, k * P:k * P + P], ident[:])
                        mm.then_inc(s["x1t_ready"], 1)
                elif what == "logits":
                    pe.wait_ge(s["x1_lo"], c * KD + KD)
                    for j in range(NT):
                        i = 0
                        for a, w in ((x1h, rwh), (x1l, rwh), (x1h, rwl)):
                            for k in range(KD):
                                mm = pe.matmul(X[0][:, j * NE:j * NE + NE], a[:, k, bass.ds(c * CH + j * P, P)],
                                               w[:, k, :], start=(i == 0), stop=(i == 5))
                                i += 1
                    mm.then_inc(s["lg_ready"], 1)
                elif what == "cT":
                    pe.wait_ge(s["c_done"], c + 1)
                    for j in range(NT):
                        mm = pe.transpose(X[0][0:NE, j * P:j * P + P], cw[:, j, :], ident[:])
                    mm.then_inc(s["cT_ready"], 1)

            def up(t, n):
                N = t * NX + n
                for bank, w, free, ready in ((G[n % 2], "g", "silu_done", "g_ready"), (U[n % 2], "u", "h_done", "u_ready")):
                    wait(pe, s[free], N - 1)
                    i = 0
                    for ww, xx in ((wh[w], x1h), (wh[w], x1l), (wl[w], x1h)):
                        for k in range(KD):
                            mm = pe.matmul(bank[:], ww[:, k, n, :], xx[:, k, bass.ds(t * CH, CH)],
                                           start=(i == 0), stop=(i == 5))
                            i += 1
                    mm.then_inc(s[ready], 1)

            def down(t, n):
                pe.wait_ge(s["lo_done"], t * NX + n + 1)
                if n == 0:
                    wait(pe, s["z2_done"], t * NT)
                for j in range(NT):
                    y = Y[j // 2][:, (j % 2) * D:(j % 2) * D + D]
                    for i, (a, w) in enumerate(((hh, wh["d"]), (hh, wl["d"]), (hl, wh["d"]))):
                        mm = pe.matmul(y, a[n % NHB][:, j * P:j * P + P], w[:, n, :],
                                       start=(n == 0 and i == 0 and j % 2 == 0),
                                       stop=(n == NX - 1 and i == 2), skip_group_check=True)
                mm.then_inc(s["down_done"], 1)

            pe.wait_ge(s["w_loaded"], 64)
            pe.wait_ge(s["rw_lo"], 1)
            for what in STEPS.values():
                step(0, what)

            def body(t, first=False, last=False):
                for n in range(NX):
                    up(t, n)
                    if n >= LAG:
                        down(t, n - LAG)
                    elif not first:
                        down(t - 1, NX - LAG + n)
                    if n in STEPS and not last:
                        step(t + 1, STEPS[n])

            body(0, first=True)
            with pe.Fori(1, NC - 1) as t:
                body(t)
            body(NC - 1, last=True)
            for n in range(NX - LAG, NX):
                down(NC - 1, n)

        @block.scalar
        def _(act):
            act.wait_ge(s["w_loaded"], 64)
            act.mul(rwh[:], rwf[:], WSC).then_inc(s["rw_hi"], 1)

            def step(c, what):
                if what == "on":
                    wait(act, s["ont_ready"], c * KD)
                    for j in range(NT):
                        mm = act.copy(On[:, j, :].rearrange("p (g n) -> p g n", g=NG), kept(c)[:, :, j, :])
                    mm.then_inc(s["on_copied"], 1)
                elif what == "ont":
                    for k in range(KD):
                        act.wait_ge(s["ont_ready"], c * KD + k + 1)
                        wait(act, s["y_ready"], c)
                        act.copy(OnT[:, k, :], X[k][:]).then_inc(s["ont_done"], 1)
                elif what == "x1t":
                    for k in range(KD):
                        act.wait_ge(s["x1t_ready"], c * KD + k + 1)
                        act.copy(x1h[:, k, bass.ds(c * CH, CH)], X[k][:]).then_inc(s["x1_hi"], 1)
                elif what == "logits":
                    act.wait_ge(s["lg_ready"], c + 1)
                    wait(act, s["c_done"], c)
                    act.activation(th[:].rearrange("p j e -> p (j e)"), X[0][:, 0:NT * NE], ACT.Tanh,
                                   scale=0.5 / WSC).then_inc(s["th_done"], 1)
                elif what == "cT":
                    act.wait_ge(s["cT_ready"], c + 1)
                    wait(act, s["cT_written"], c * 16)
                    act.copy(cT[:], X[0][0:NE, :]).then_inc(s["cT_done"], 1)

            def silu(t, n):
                N = t * NX + n
                act.wait_ge(s["g_ready"], N + 1)
                wait(act, s["h_done"], N - 1)
                act.activation(sg[n % 2][:], G[n % 2][:], ACT.Silu, scale=1.0 / WSC).then_inc(s["silu_done"], 1)

            def high(t, n):
                N = t * NX + n
                act.wait_ge(s["h_done"], N + 1)
                wait(act, s["down_done"], N - NHB + 1)
                act.copy(hh[n % NHB][:], hf[n % 2][:]).then_inc(s["hi_done"], 1)

            for what in STEPS.values():
                step(0, what)

            def body(t, last=False):
                for n in range(NX):
                    silu(t, n)
                    high(t, n)
                    if n in STEPS and not last:
                        step(t + 1, STEPS[n])

            body(0)
            with act.Fori(1, NC - 1) as t:
                body(t)
            body(NC - 1, last=True)

        @block.vector
        def _(dve):
            dve.wait_ge(s["rw_hi"], 1)
            dve.scalar_tensor_tensor(rwl[:], rwf[:], WSC, rwh[:], op0=ALU.mult, op1=ALU.subtract)\
               .then_inc(s["rw_lo"], 1)
            dve.wait_ge(s["consts"], 3)

            def variance(w, c, z_done, per, stats_done, var_done):
                for j in range(NT):
                    dve.wait_ge(z_done, c * per + j // (NT // per) + 1)
                    dve.bn_stats(st[w][:, j, :], zz[w][:, j, :]).then_inc(stats_done, 1)
                for j in range(NT):
                    dve.wait_ge(stats_done, c * NT + j + 1)
                    settle(dve, s["settled"])
                    dve.bn_aggr(mv[w][:, j, :], st[w][:, j, :]).then_inc(var_done, 1)

            def norm(w, dst, ready):
                for j in range(NT):
                    dve.tensor_scalar(dst[:, j, :], zz[w][:, j, :], mv[w][:, j, 0:1], rstd[w][:, j:j + 1],
                                      op0=ALU.subtract, op1=ALU.mult).then_inc(ready, 1)

            def step(c, what):
                if what == "y":
                    dve.wait_ge(s["y_ready"], c + 1)
                    dve.wait_ge(s["xb_done"], c + 1)
                    for i in range(2):
                        dve.tensor_tensor(zz[0][:, 2 * i:2 * i + 2, :].rearrange("p j n -> p (j n)"), X[i][:],
                                          xb[:, 2 * i:2 * i + 2, :].rearrange("p j n -> p (j n)"), op=ALU.add)\
                           .then_inc(s["z_done"], 1)
                elif what == "var":
                    variance(0, c, s["z_done"], 2, s["stats_done"], s["var_done"])
                elif what == "norm":
                    dve.wait_ge(s["rstd_done"], c + 1)
                    wait(dve, s["x1_kept"], c)
                    norm(0, x1c, s["x1_done"])
                elif what == "x1t":
                    for k in range(KD):
                        dve.wait_ge(s["x1_hi"], c * KD + k + 1)
                        dve.tensor_tensor(x1l[:, k, bass.ds(c * CH, CH)], X[k][:], x1h[:, k, bass.ds(c * CH, CH)],
                                          op=ALU.subtract).then_inc(s["x1_lo"], 1)
                elif what[:-1] == "route":
                    route(c, int(what[-1]))

            FROM = [0, 7, 13, 20, 22, 30]

            def route(c, part):
                done = [FROM[part]]

                def link(ins):
                    done[0] += 1
                    ins.then_inc(s["route_step"], 1)
                    dve.wait_ge(s["route_step"], c * FROM[-1] + done[0])

                s4 = sc[:].rearrange("p t (g e) -> p t g e", e=4)
                pairs = [(a, b) for a in range(4) for b in range(a + 1, 4)]
                if part == 0:
                    dve.wait_ge(s["th_done"], c + 1)
                    link(dve.tensor_scalar(th[:], th[:], 0.5, 0.5, op0=ALU.mult, op1=ALU.add))
                    link(dve.tensor_tensor(sc[:], th[:], eb[:].unsqueeze(1).to_broadcast([P, NT, NE]), op=ALU.add))
                    link(dve.tensor_tensor(pr[0][:], s4[:, :, :, 0], s4[:, :, :, 1], op=ALU.add))
                    for a, b in pairs[1:3]:
                        link(dve.tensor_tensor(pr[1][:], s4[:, :, :, a], s4[:, :, :, b], op=ALU.add))
                        link(dve.tensor_tensor(pr[0][:], pr[0][:], pr[1][:], op=ALU.max))
                elif part == 1:
                    for a, b in pairs[3:]:
                        link(dve.tensor_tensor(pr[1][:], s4[:, :, :, a], s4[:, :, :, b], op=ALU.add))
                        link(dve.tensor_tensor(pr[0][:], pr[0][:], pr[1][:], op=ALU.max))
                elif part == 2:
                    g4 = pr[0][:]
                    gg, ge = gt[:, :, 0:4, 0:4], eq[:, :, 0:4, 0:4]
                    one = g4.unsqueeze(2).to_broadcast([P, NT, 4, 4])
                    two = g4.unsqueeze(3).to_broadcast([P, NT, 4, 4])
                    link(dve.tensor_tensor(gg, one, two, op=ALU.is_gt))
                    link(dve.tensor_tensor(ge, one, two, op=ALU.is_equal))
                    link(dve.tensor_tensor(ge, ge, tri[:, 0:4, 0:4].unsqueeze(1).to_broadcast([P, NT, 4, 4]),
                                           op=ALU.mult))
                    link(dve.tensor_tensor(gg, gg, ge, op=ALU.add))
                    link(dve.tensor_reduce(rk[:], gg, AX.X, ALU.add))
                    link(dve.tensor_scalar(rk[:], rk[:], 2.0, None, op0=ALU.is_lt))
                    v4 = vm[:].rearrange("p t (g e) -> p t g e", e=4)
                    link(dve.tensor_tensor(v4, s4, rk[:].unsqueeze(3).to_broadcast([P, NT, 4, 4]), op=ALU.mult))
                elif part == 3:
                    one = vm[:].unsqueeze(2).to_broadcast([P, NT, NE, NE])
                    two = vm[:].unsqueeze(3).to_broadcast([P, NT, NE, NE])
                    link(dve.tensor_tensor(gt[:], one, two, op=ALU.is_gt))
                    link(dve.tensor_tensor(eq[:], one, two, op=ALU.is_equal))
                else:
                    link(dve.tensor_tensor(eq[:], eq[:], tri[:].unsqueeze(1).to_broadcast([P, NT, NE, NE]),
                                           op=ALU.mult))
                    link(dve.tensor_tensor(gt[:], gt[:], eq[:], op=ALU.add))
                    link(dve.tensor_reduce(rank[:], gt[:], AX.X, ALU.add))
                    link(dve.scalar_tensor_tensor(vm[:], rank[:], float(TOPK), th[:], op0=ALU.is_lt, op1=ALU.mult))
                    link(dve.tensor_reduce(tot[:], vm[:], AX.X, ALU.add))
                    link(dve.tensor_scalar(tot[:], tot[:], 1e-20, None, op0=ALU.add))
                    link(dve.reciprocal(tot[:], tot[:]))
                    link(dve.tensor_tensor(vm[:], vm[:], tot[:].unsqueeze(2).to_broadcast([P, NT, NE]), op=ALU.mult))
                    wait(dve, s["cT_ready"], c)
                    dve.tensor_scalar(cw[:], vm[:], 2.5, None, op0=ALU.mult).then_inc(s["c_done"], 1)
                assert done[0] == (FROM + [0])[part + 1], done

            def gated(t, n):
                N = t * NX + n
                dve.wait_ge(s["silu_done"], N + 1)
                if n >= NSH:
                    e = n - NSH
                    dve.wait_ge(c_loaded[e % NCB], (t * (NE // NCB) + e // NCB) * 16 + 16)
                    dve.tensor_tensor(sg[n % 2][:], sg[n % 2][:], cb[e % NCB][:], op=ALU.mult).then_inc(s["sc_done"], 1)
                    dve.wait_ge(s["sc_done"], t * NE + e + 1)
                dve.wait_ge(s["u_ready"], N + 1)
                wait(dve, s["lo_done"], N - 1)
                wait(dve, s["hi_done"], N - 1)
                dve.scalar_tensor_tensor(hf[n % 2][:], U[n % 2][:], 1.0 / WSC, sg[n % 2][:],
                                         op0=ALU.mult, op1=ALU.mult).then_inc(s["h_done"], 1)

            def low(t, n):
                N = t * NX + n
                dve.wait_ge(s["hi_done"], N + 1)
                wait(dve, s["down_done"], N - NHB + 1)
                dve.tensor_tensor(hl[n % NHB][:], hf[n % 2][:], hh[n % NHB][:], op=ALU.subtract)\
                   .then_inc(s["lo_done"], 1)

            def residual(t):
                dve.wait_ge(s["down_done"], t * NX + NX)
                dve.wait_ge(s["x1_kept"], t + 1)
                for j in range(NT):
                    y = Y[j // 2][:, (j % 2) * D:(j % 2) * D + D].rearrange("p (g n) -> p g n", g=NG)
                    dve.scalar_tensor_tensor(zz[1][:, j, :].rearrange("p (g n) -> p g n", g=NG), y, 1.0 / WSC,
                                             kept(t)[:, :, j, :], op0=ALU.mult, op1=ALU.add).then_inc(s["z2_done"], 1)

            def finish(t, n):
                if n == LAG:
                    residual(t)
                elif n == LAG + 1:
                    variance(1, t, s["z2_done"], NT, s["stats2_done"], s["var2_done"])
                elif n == LAG + 3:
                    dve.wait_ge(s["rstd2_done"], t + 1)
                    wait(dve, s["out_written"], t * 16)
                    norm(1, oo, s["out_ready"])

            for what in STEPS.values():
                step(0, what)

            def body(t, first=False, last=False):
                for n in range(NX):
                    if not first:
                        finish(t - 1, n)
                    gated(t, n)
                    low(t, n)
                    if n in STEPS and not last:
                        step(t + 1, STEPS[n])

            body(0, first=True)
            with dve.Fori(1, NC - 1) as t:
                body(t)
            body(NC - 1, last=True)
            for n in range(NX):
                finish(NC - 1, n)


def halves_first(a):
    return a.reshape(B, NH2, CH, D).swapaxes(0, 1).reshape(T, D)


def kernel(**inputs):
    import numpy as np
    import concourse.bacc as bacc
    from concourse.bass_utils import run_bass_kernel_spmd

    g = {k: np.asarray(v) for k, v in inputs.items()}
    x = g["L0_attn_x"].reshape(T, D)

    def by_dim(a):
        return a.reshape(NG, HG, HD, *a.shape[1:]).swapaxes(1, 2).reshape(a.shape)

    def by_pair(a):
        return a.reshape(NG, 2, 2, HD, *a.shape[1:]).swapaxes(2, 3).reshape(a.shape)

    w, b = g["L0_attn_in_proj_w"].reshape(3, D, D), g["L0_attn_in_proj_b"].reshape(3, D)
    arrays = {
        "x": halves_first(x),
        "xT": x.T,
        "winT": np.concatenate([by_pair(w[0]), by_pair(w[1]), by_dim(w[2])]).T,
        "bqkT": np.concatenate([by_pair(b[0]), by_pair(b[1])]).reshape(2 * KD, P).T,
        "bvr": by_dim(b[2]),
        "woutT": g["L0_attn_out_proj_w"].T,
        "bout": g["L0_attn_out_proj_b"],
        "rwT": g["L0_ffn_router_weight"].T,
        "ebias": g["L0_ffn_e_bias"],
        "gwT": g["L0_ffn_gate_w"].transpose(2, 0, 1),
        "uwT": g["L0_ffn_up_w"].transpose(2, 0, 1),
        "dwT": g["L0_ffn_down_w"].transpose(2, 0, 1),
        "sgT": g["L0_ffn_sh_gate_w"].T,
        "suT": g["L0_ffn_sh_up_w"].T,
        "sdT": g["L0_ffn_sh_down_w"].T,
    }
    nc = bacc.Bacc("TRN2", target_bir_lowering=False, num_devices=1)
    ins = {}
    for name, a in list(arrays.items()):
        a = np.ascontiguousarray(a)
        arrays[name] = a
        ins[name] = nc.dram_tensor(name, a.shape, mybir.dt.from_np(a.dtype), kind="ExternalInput").ap()
    out = nc.dram_tensor("out", (T, D), F32, kind="ExternalOutput").ap()
    attention_moe(nc, **ins, out=out)
    r = run_bass_kernel_spmd(nc, [arrays], core_ids=[0])
    return r.results[0]["out"].reshape(NH2, B, CH, D).swapaxes(0, 1).reshape(B, S, D)
```

```python
import concourse.bass as bass
from concourse import mybir
from contextlib import ExitStack

F32 = mybir.dt.float32
F16 = mybir.dt.float16
ALU = mybir.AluOpType
ACT = mybir.ActivationFunctionType
AX = mybir.AxisListType

P = 128
B, S, D = 4, 1024, 256
T = B * S
H, HD = 16, 16
WIN = 64
NE, I, NSH, TOPK = 16, 128, 2, 4
NX = NE + NSH
EPS = 1e-5
CH = 512
NC = T // CH
NT = CH // P
KD = D // P
NH2 = S // CH
WSC = 64.0
BIG = 32768.0

NCB, NHB = 4, 3
HG = 4
NG = H // HG
NR = B * NG
VW = HG * (HD + 1)
MR = 112
SLOTS = [(qc, kt, max(qc * CH, kt * P - WIN)) for qc in range(NH2) for kt in range(S // P)
         if kt * P - WIN < (qc + 1) * CH]
NSL = len(SLOTS)


def max_units():
    units = []
    for t in range(S // P):
        w = min(P * t + P + WIN, S)
        for piece, (lo, hi) in enumerate([(0, min(w, CH)), (CH, w)]):
            if hi > lo:
                n = {1: 1, 2: 2, 3: 2}.get(CH // (hi - lo), HG)
                units += [(t, piece, lo, hi, range(h, h + n)) for h in range(0, HG, n)]
    return units


UNITS = max_units()
NU = len(UNITS)
NEEDS = [0, next(u for u, (t, _, _, hi, _) in enumerate(UNITS) if t * P >= CH or hi > CH)]
SECOND = next(u for u, (t, *_) in enumerate(UNITS) if t * P >= CH)
TAIL = 4
FIXED = 256


def share(slot):
    cols = [(qc + 1) * CH - q0 + FIXED for qc, _, q0 in SLOTS]
    lo, hi = (NU * sum(cols[:n]) // sum(cols) for n in (slot, slot + 1))
    return [((n - TAIL) % NU, n >= TAIL) for n in range(lo, hi)]


def settle(eng, sem):
    eng.sem_inc(sem, 1)


def wait(eng, sem, value):
    if not (isinstance(value, int) and value <= 0):
        eng.wait_ge(sem, value)


def rounds(eng, n, body):
    body(0, 0, 0)
    body(1, 1, 0)
    with eng.Fori(1, n // 2 - 1) as i:
        body(i * 2, 0, i)
        body(i * 2 + 1, 1, i)
    body(n - 2, 0, n // 2 - 1)
    body(n - 1, 1, n // 2 - 1, last=True)


def attention_moe(nc, x, xT, winT, bqkT, bvr, woutT, bout, rwT, ebias, gwT, uwT, dwT, sgT, suT, sdT, out):
    with ExitStack() as ctx:
        q_dram = nc.dram_tensor("q_dram", [2, B * D // 2, NH2, 2, CH], F16).ap()
        k_dram = nc.dram_tensor("k_dram", [2, B * D // 2, NH2, 2, CH], F16).ap()
        c_dram = nc.dram_tensor("c_dram", [NE, T], F32).ap()
        banks = [ctx.enter_context(nc.psum_tensor(f"bank{i}", [P, CH], F32)) for i in range(8)]

        def keep(name, shape, dt):
            return ctx.enter_context(nc.sbuf_tensor(name, shape, dt))

        def opener(where, prefix):
            def sb(name, shape, dt):
                return where.enter_context(nc.sbuf_tensor(prefix + name, shape, dt))
            return sb

        ident = keep("ident", [P, P], F32)
        with ExitStack() as st:
            proj = projection_memory(opener(st, "p_"))
        o_all = keep("o_all", [P, NH2, NR, NT, HG * HD], F32)
        wh, wl = ({"g": keep("g" + part, [P, KD, NX, I], F16), "u": keep("u" + part, [P, KD, NX, I], F16),
                   "d": keep("d" + part, [P, NX, D], F16)} for part in "hl")
        norms = norm_memory(keep)
        with ExitStack() as st:
            att = attention_memory(opener(st, "a_"))
        exps = expert_memory(keep)
        program(nc, ctx, banks, ident, proj, att, norms, exps, o_all, wh, wl, q_dram, k_dram, c_dram, x, xT, winT,
                bqkT, bvr, woutT, bout, rwT, ebias, gwT, uwT, dwT, sgT, suT, sdT, out)


def projection_memory(sb):
    stage = sb("stage", [P, KD, 3 * D], F32)
    winh = sb("winh", [P, KD, 3 * D], F16)
    winl = sb("winl", [P, KD, 3 * D], F16)
    bqk = sb("bqk", [P, 4], F32)
    bqs = sb("bqs", [P, 4], F32)
    bv = sb("bv", [P, NG, HG * HD], F32)
    xf = [sb(f"xf{p}", [P, KD, CH], F32) for p in range(2)]
    xh = [sb(f"xh{p}", [P, KD, CH], F16) for p in range(2)]
    xl = [sb(f"xl{p}", [P, KD, CH], F16) for p in range(2)]
    qkf = [sb(f"qkf{m}", [P, CH], F32) for m in range(4)]
    qk16 = [sb(f"qk16{p}", [P, 2, 4, CH], F16) for p in range(2)]
    return xf, xh, xl, qkf, qk16, stage, winh, winl, bqk, bqs, bv


def norm_memory(sb):
    wo = sb("wo", [P, KD, D], F32)
    woh = sb("woh", [P, KD, D], F16)
    wol = sb("wol", [P, KD, D], F16)
    rwf = sb("rwf", [P, KD, NE], F32)
    rwh = sb("rwh", [P, KD, NE], F16)
    rwl = sb("rwl", [P, KD, NE], F16)
    bo = sb("bo", [P, D], F32)
    eb = sb("eb", [P, NE], F32)
    On = sb("On", [P, NT, D], F32)
    Oh = sb("Oh", [P, KD, CH], F16)
    Ol = sb("Ol", [P, KD, CH], F16)
    xb = sb("xb", [P, NT, D], F32)
    x1c = sb("x1c", [P, NT, D], F32)
    z1 = sb("z1", [P, NT, D], F32)
    st, mv, ve, rstd = ([sb(f"{n}{w}", [P, *shape], F32) for w in range(2)] for n, shape in
                            (("st", (NT, 6)), ("mv", (NT, 2)), ("ve", (NT,)), ("rstd", (NT,))))
    mhalf = sb("mhalf", [P, NT], F32)
    th = sb("th", [P, NT, NE], F32)
    sc = sb("sc", [P, NT, NE], F32)
    vm = sb("vm", [P, NT, NE], F32)
    pr = [sb(f"pr{i}", [P, NT, 4], F32) for i in range(2)]
    rk = sb("rk", [P, NT, 4], F32)
    gt = sb("gt", [P, NT, NE, NE], F16)
    eq = sb("eq", [P, NT, NE, NE], F16)
    lower = sb("lower", [P, NE, NE], F16)
    rank = sb("rank", [P, NT, NE], F32)
    tot = sb("tot", [P, NT], F32)
    cw = sb("cw", [P, NT, NE], F32)
    cT = sb("cT", [NE, CH], F32)
    return (wo, woh, wol, rwf, rwh, rwl, bo, eb, On, Oh, Ol, xb, x1c, z1, st, mv, ve, rstd, mhalf,
            th, sc, vm, pr, rk, gt, eq, lower, rank, tot, cw, cT)


def attention_memory(sb):
    v_all = sb("v_all", [P, NR, S // P, VW], F32)
    QS = [sb(f"QS{p}", [P, NH2, HG, CH], F16) for p in range(2)]
    KS = [sb(f"KS{p}", [P, NH2, HG // 2, CH], F16) for p in range(2)]
    VG = [sb(f"VG{p}", [P, S // P, VW], F32) for p in range(2)]
    idb = sb("idb", [P, P], F16)
    tri = sb("tri", [P, P], F16)
    mx = sb("mx", [P, 2, NH2, HG, NT], F32)
    mT = [sb(f"mT{half}", [HG * NT, P], F16) for half in range(NH2)]
    OTs = sb("OTs", [P, CH], F32)
    rec = sb("rec", [P, NT, HG], F32)
    raw = [sb(f"raw{p}", [P, 2 * KD * I + D], F32) for p in range(2)]
    PT = [sb(f"PT{p}", [P, HG, CH], F32) for p in range(2)]
    return v_all, QS, KS, VG, idb, tri, mx, mT, OTs, rec, raw, PT


def expert_memory(sb):
    x1h = sb("x1h", [P, KD, T], F16)
    x1l = sb("x1l", [P, KD, T], F16)
    cb = [sb(f"cb{i}", [P, CH], F32) for i in range(NCB)]
    sg = [sb(f"sg{i}", [P, CH], F32) for i in range(2)]
    hf = [sb(f"hf{i}", [P, CH], F32) for i in range(2)]
    hh = [sb(f"hh{i}", [P, CH], F16) for i in range(NHB)]
    hl = [sb(f"hl{i}", [P, CH], F16) for i in range(NHB)]
    z2 = sb("z2", [P, NT, D], F32)
    oo = sb("oo", [P, NT, D], F32)
    return x1h, x1l, cb, sg, hf, hh, hl, z2, oo


def program(nc, ctx, banks, ident, proj, att, norms, exps, o_all, wh, wl, q_dram, k_dram, c_dram, x, xT, winT,
            bqkT, bvr, woutT, bout, rwT, ebias, gwT, uwT, dwT, sgT, suT, sdT, out):
    def sems(names, prefix):
        return {n: ctx.enter_context(nc.semaphore(prefix + n)) for n in names.split()}

    xf, xh, xl, qkf, qk16, stage, winh, winl, bqk, bqs, bv = proj
    v_all, QS, KS, VG, idb, tri, mx, mT, OTs, rec, raw, PT = att
    (wo, woh, wol, rwf, rwh, rwl, bo, eb, On, Oh, Ol, xb, x1c, z1, st, mv, ve, rstd, mhalf,
     th, sc, vm, pr, rk, gt, eq, lower, rank, tot, cw, cT) = norms
    x1h, x1l, cb, sg, hf, hh, hl, z2, oo = exps
    zz = [z1, z2]
    pre = sems("""w_loaded0 w_loaded1 b_loaded w_hi w_lo bias_done ident_zero ident_done ones_done x_loaded0
        x_loaded1 x_hi x_split proj_ready qk_f32 qk_hi qk_lo v_done qk_written0 qk_written1""", "p_")
    x_loaded = [pre["x_loaded0"], pre["x_loaded1"]]
    qk_written = [pre["qk_written0"], pre["qk_written1"]]
    s = sems("""zeroed stack_zero tri_done stack_const otb_zero stacked00 stacked01 stacked10 stacked11
        negmax00 negmax01 negmax10 negmax11 v_copied s_ready masked max_done both_max mT_ready
        mT_done st_ready exp_done pv_done ot_done ott_ready rec_done o_done raw_loaded0 raw_loaded1 w_hi w_lo settled""", "a_")
    f = sems("""w_loaded consts rw_hi rw_lo on_copied ont_ready ont_hi ont_done xb_loaded xb_done y_ready z_done
        stats_done var_done eps_done rstd_done x1_done x1t_ready x1_hi x1_lo x1_kept lg_ready th_done route_step
        c_done cT_ready cT_done cT_written g_ready u_ready silu_done sc_done h_done hi_done lo_done down_done
        z2_done stats2_done var2_done eps2_done rstd2_done out_ready out_written""", "e_")
    c_loaded = list(sems(" ".join(f"c_loaded{i}" for i in range(NCB)), "e_").values())
    stacked = [[s[f"stacked{half}{p}"] for p in range(2)] for half in range(NH2)]
    negmax = [[s[f"negmax{half}{p}"] for p in range(2)] for half in range(NH2)]
    raw_loaded = [s["raw_loaded0"], s["raw_loaded1"]]
    NM = 6
    pbank = [banks[3 + m % 2] for m in range(4)] + banks[5:7]
    FIRST_S = [[range(*((NU - TAIL) * (n * NM + m + d) // (2 * NM) for d in range(2))) for m in range(NM)]
               for n in range(2)]
    sbank, stbank, otbank, aux = banks[0:3], banks[3:6], banks[6], banks[7]
    NRAW = 2 * KD + 1
    NST = NSL * HG
    LAST_OF = [max(u for u in range(NST) if u % 3 == n) for n in range(3)]
    HALF = [max(i for i, sl in enumerate(SLOTS) if sl[0] == qc) for qc in range(NH2)]
    MASKED = [i for i, (_, kt, q0) in enumerate(SLOTS) if kt * P + WIN > q0]
    FIRST = 1 + max(i for i, (qc, kt, _) in enumerate(SLOTS) if qc == 0 or kt < CH // P)
    MAXT, OTT = [FIRST, 1], [HALF[0] + 3, 2]

    gbank, ubank, ybank = banks[0:2], banks[2:4], banks[4:6]

    def nbank(c):
        return banks[0:2] if isinstance(c, int) and c == 0 else banks[6:8]

    LAG = 2

    def kept(c):
        return o_all[:].rearrange("p h (b g) j n -> p (h b) g j n", g=NG)[:, bass.ds(c, 1)].squeeze(1)

    def tiles(a):
        return a[:].rearrange("p j (g n) -> p g j n", g=NG)

    STEPS0 = {2: ["on"], 3: ["ont"], 4: ["y"], 5: ["var"], 6: ["norm"], 7: ["x1t"], 8: ["logits"], 9: ["route0"],
              10: ["route1"], 11: ["route2", "route3"], 12: ["route4"]}
    STEPS = {1: "on", 2: "ont", 3: "y", 4: "var", 6: "norm", 7: "x1t", 8: "logits", 9: "route0", 10: "route1",
             11: "route2", 12: "route3", 13: "route4", 15: "cT"}

    def first_scores(c, m):
        return FIRST_S[c - NC + 2][m] if isinstance(c, int) and c >= NC - 2 else ()

    def parts(w):
        return (w[:, 0:KD * I].rearrange("p (k i) -> p k i", k=KD),
                w[:, KD * I:2 * KD * I].rearrange("p (k i) -> p k i", k=KD), w[:, 2 * KD * I:])

    def split_of(w, n):
        return (w["g"][:, :, bass.ds(n, 1), :].squeeze(2), w["u"][:, :, bass.ds(n, 1), :].squeeze(2),
                w["d"][:, bass.ds(n, 1), :].squeeze(1))

    with nc.Block() as block:

        @block.sync
        def _(sp):
            def load_x(c, p):
                sp.dma_start(xf[p][:], xT[:, bass.ds(c * CH, CH)].rearrange("(k p) t -> p k t", p=P))\
                  .then_inc(x_loaded[p], 16)

            load_x(0, 0)
            for k in range(KD):
                sp.dma_start(stage[:, k, :], winT.rearrange("(k p) n -> p k n", p=P)[:, k])\
                  .then_inc(pre[f"w_loaded{k}"], 16)
            sp.dma_start(bqk[:], bqkT).then_inc(pre["b_loaded"], 16)
            sp.dma_start(bv[:].rearrange("p g n -> p (g n)"), bvr.partition_broadcast(P))\
              .then_inc(pre["b_loaded"], 16)
            load_x(1, 1)

            def project(c, p, k, last=False):
                sp.wait_ge(pre["qk_lo"], c * 4 + 4)
                settle(sp, s["settled"])
                for part in range(2):
                    for m in range(4):
                        dst = (q_dram, k_dram)[m // 2][part, bass.ds(k * (D // 2) + (m % 2) * HD * HG, HD * HG), p]
                        sp.dma_start(dst, qk16[p][:, part, m, :]).then_inc(qk_written[p], 16)

            def stack(G, p, half):
                for e in range(2):
                    for dst, src, n, both_at, one_at in ((QS[p], q_dram, HG // 2, 0, 2 * HD),
                                                         (KS[p], k_dram, 0, HD, 0)):
                        a = src[:, bass.ds(G * (2 * HD) + e * HD, HD), half].rearrange("s d i t -> s d (i t)")
                        to = dst[:, half, n * e:n * e + 2, :].rearrange("p i t -> p (i t)")
                        at = 64 * e + both_at
                        sp.dma_start(to[at:at + 2 * HD], a).then_inc(stacked[half][p], 16)
                        at = 64 * e + one_at
                        sp.dma_start(to[at:at + HD], a[0]).then_inc(stacked[half][p], 16)

            def load_raw(n, p):
                wait(sp, s["w_lo"], (n - 1) * 3)
                g, u, d = parts(raw[p])
                if isinstance(n, int) and n < NSH:
                    gs, us = (a.rearrange("(k p) (e i) -> k p e i", p=P, i=I)[:, :, n, :] for a in (sgT, suT))
                    src = sdT.rearrange("(e i) n -> e i n", i=I)[n]
                else:
                    gs, us = (a[:, bass.ds(n - NSH, 1), :].squeeze(1).rearrange("(k p) i -> k p i", p=P)
                              for a in (gwT, uwT))
                    src = dwT[:, bass.ds(n - NSH, 1), :].squeeze(1)
                for kk in range(KD):
                    sp.dma_start(g[:, kk, :], gs[kk]).then_inc(raw_loaded[p], 16)
                    sp.dma_start(u[:, kk, :], us[kk]).then_inc(raw_loaded[p], 16)
                sp.dma_start(d, src).then_inc(raw_loaded[p], 16)

            def put_max(G, p, half):
                sp.wait_ge(s["mT_done"], G * NH2 + half + 1)
                sp.dma_start(QS[p][MR:MR + 1, half, :, :].rearrange("o h t -> o (h t)"), mT[half][:])\
                  .then_inc(negmax[half][p], 16)

            project(0, 0, 0)
            project(1, 1, 0)
            sp.dma_start(wo[:], woutT.rearrange("(k p) n -> p k n", p=P)).then_inc(f["w_loaded"], 16)
            sp.dma_start(rwf[:], rwT.rearrange("(k p) n -> p k n", p=P)).then_inc(f["w_loaded"], 16)
            sp.dma_start(bo[:], bout.partition_broadcast(P)).then_inc(f["w_loaded"], 16)
            sp.dma_start(eb[:], ebias.partition_broadcast(P)).then_inc(f["w_loaded"], 16)
            for p in range(2):
                sp.wait_ge(qk_written[p], 128)
            sp.wait_ge(s["stack_const"], 4)
            stack(0, 0, 0)
            with sp.Fori(1, NC // 2 - 1) as i:
                project(i * 2, 0, i)
                project(i * 2 + 1, 1, i)
            stack(0, 0, 1)
            for n in range(NSH):
                load_raw(n, n)
            project(NC - 2, 0, NC // 2 - 1)
            put_max(0, 0, 0)
            project(NC - 1, 1, NC // 2 - 1, last=True)
            for p in range(2):
                sp.wait_ge(qk_written[p], 128 * (NC // 2))
            stack(1, 1, 0)
            stack(1, 1, 1)

            def body(G, p, k, last=False):
                more = not (isinstance(G, int) and G >= NR - 2)
                put_max(G, p, 1)
                load_raw(G + NSH, p)
                if more:
                    sp.wait_ge(s["st_ready"], G * NST + FIRST * HG)
                    stack(G + 2, p, 0)
                if not last:
                    put_max(G + 1, 1 - p, 0)
                if more:
                    sp.wait_ge(s["st_ready"], G * NST + NST)
                    stack(G + 2, p, 1)

            rounds(sp, NR, body)

            def load_xb(c):
                wait(sp, f["z_done"], c * 2)
                sp.dma_start(xb[:], x[bass.ds(c * CH, CH), :].rearrange("(j p) n -> p j n", p=P))\
                  .then_inc(f["xb_loaded"], 16)

            def store_c(c):
                sp.wait_ge(f["cT_done"], c + 1)
                sp.dma_start(c_dram[:, bass.ds(c * CH, CH)], cT[:]).then_inc(f["cT_written"], 16)

            def load_c(t, e):
                if e == 0:
                    sp.wait_ge(f["cT_written"], t * 16 + 16)
                    settle(sp, s["settled"])
                wait(sp, f["sc_done"], t * NE + e - NCB + 1)
                sp.dma_start(cb[e % NCB][:], c_dram[e, bass.ds(t * CH, CH)].partition_broadcast(P))\
                  .then_inc(c_loaded[e % NCB], 16)

            def chunk(t, first=False, last=False):
                for e in range(NE):
                    load_c(t, e)
                    if e == 8 and not first:
                        sp.wait_ge(f["out_ready"], t * NT)
                        sp.dma_start(out[bass.ds((t - 1) * CH, CH), :].rearrange("(j p) n -> p j n", p=P), oo[:])\
                          .then_inc(f["out_written"], 16)
                    if e == 4 and not (isinstance(t, int) and t >= NC - 2):
                        load_xb(t + 2)
                    if e == NE - 1 and not last:
                        store_c(t + 1)

            load_xb(0)
            load_xb(1)
            store_c(0)
            sp.wait_ge(s["pv_done"], NR * NSL)
            sp.wait_ge(s["o_done"], NR * NH2)
            sp.wait_ge(s["w_lo"], NX * 3)
            chunk(0, first=True)
            with sp.Fori(1, NC - 2) as t:
                chunk(t)
            chunk(NC - 2)
            chunk(NC - 1, last=True)
            sp.wait_ge(f["out_ready"], NC * NT)
            sp.dma_start(out[(NC - 1) * CH:, :].rearrange("(j p) n -> p j n", p=P), oo[:])\
              .then_inc(f["out_written"], 16)
            sp.wait_ge(f["out_written"], 16 * NC)

        @block.gpsimd
        def _(pool):
            pool.memset(idb[:], 0.0).then_inc(s["zeroed"], 1)
            pool.memset(tri[:], 0.0).then_inc(s["zeroed"], 1)
            pool.wait_ge(s["zeroed"], 2)
            pool.affine_select(out=idb[:], in_=idb[:], compare_op=ALU.not_equal, fill=BIG, base=0,
                               pattern=[[-1, P]], channel_multiplier=1).then_inc(s["tri_done"], 1)
            pool.affine_select(out=tri[:], in_=tri[:], compare_op=ALU.is_ge, fill=-BIG, base=0,
                               pattern=[[-1, P]], channel_multiplier=1).then_inc(s["tri_done"], 1)

            pool.memset(ident[:], 0.0).then_inc(pre["ident_zero"], 1)
            pool.memset(v_all[:, :, :, HG * HD:VW], 1.0).then_inc(pre["ones_done"], 1)
            pool.wait_ge(pre["ident_zero"], 1)
            pool.affine_select(out=ident[:], in_=ident[:], compare_op=ALU.not_equal, fill=1.0, base=0,
                               pattern=[[-1, P]], channel_multiplier=1).then_inc(pre["ident_done"], 1)

            for a in (KS[0], KS[1]):
                pool.memset(a[:], 0.0).then_inc(s["stack_zero"], 1)

            def split_x(c, p):
                pool.wait_ge(pre["x_hi"], c + 1)
                settle(pool, s["settled"])
                pool.tensor_tensor(xl[p][:], xf[p][:], xh[p][:], op=ALU.subtract).then_inc(pre["x_split"], 1)

            def project(c, p, k, last=False):
                if not last:
                    split_x(c + 1, 1 - p)
                for m in range(4):
                    pool.wait_ge(pre["qk_hi"], c * 4 + m + 1)
                    pool.tensor_tensor(qk16[p][:, 1, m, :], qkf[m][:], qk16[p][:, 0, m, :], op=ALU.subtract)\
                        .then_inc(pre["qk_lo"], 1)

            split_x(0, 0)
            rounds(pool, NC, project)

            pool.memset(mhalf[:], -0.5).then_inc(f["consts"], 1)
            pool.memset(lower[:], 1.0).then_inc(f["consts"], 1)
            pool.wait_ge(f["consts"], 2)
            pool.affine_select(out=lower[:], in_=lower[:], compare_op=ALU.is_gt, fill=0.0, base=0,
                               pattern=[[1, NE], [-1, NE]], channel_multiplier=0).then_inc(f["consts"], 1)

            pool.wait_ge(pre["ones_done"], 1)

            def copy_v(G, p):
                wait(pool, s["pv_done"], (G - 1) * NSL)
                settle(pool, s["settled"])
                pool.tensor_copy(VG[p][:], v_all[:, bass.ds(G, 1), :, :].squeeze(1)).then_inc(s["v_copied"], 1)

            def mask(G, p, i):
                qc, kt, q0 = SLOTS[i]
                w = min((qc + 1) * CH, kt * P + WIN) - q0
                for h in range(0, HG, 2):
                    pool.wait_ge(s["exp_done"], G * NST + i * HG + h + 2)
                    settle(pool, s["settled"])
                    a = PT[(p + i) % 2][:, h:h + 2, 0:w]
                    pool.affine_select(out=a, in_=a, compare_op=ALU.is_ge, fill=0.0, base=q0 - (kt * P - WIN),
                                       pattern=[[0, 2], [1, w]], channel_multiplier=-1).then_inc(s["masked"], 1)

            pool.wait_ge(f["w_loaded"], 64)

            def add_bo(c):
                pool.wait_ge(f["xb_loaded"], c * 16 + 16)
                for j in range(NT):
                    last_ = pool.tensor_tensor(xb[:, j, :], xb[:, j, :], bo[:], op=ALU.add)
                last_.then_inc(f["xb_done"], 1)

            def rstd_(w, c, var, eps, done):
                pool.wait_ge(var, c * NT + NT)
                settle(pool, s["settled"])
                pool.tensor_scalar(ve[w][:], mv[w][:, :, 1], EPS, None, op0=ALU.add).then_inc(eps, 1)
                pool.wait_ge(eps, c + 1)
                pool.tensor_tensor(rstd[w][:], ve[w][:], mhalf[:], op=ALU.pow).then_inc(done, 1)

            def first_norm(c):
                rstd_(0, c, f["var_done"], f["eps_done"], f["rstd_done"])
                pool.wait_ge(f["x1_done"], c * NT + NT)
                settle(pool, s["settled"])
                pool.tensor_copy(kept(c), tiles(x1c)).then_inc(f["x1_kept"], 1)

            def second_norm(t):
                rstd_(1, t, f["var2_done"], f["eps2_done"], f["rstd2_done"])

            def body(G, p, k, last=False):
                for i in MASKED:
                    mask(G, p, i)
                    if i == 2 and not last:
                        copy_v(G + 1, 1 - p)
                    if i == HALF[0] and last:
                        add_bo(0)
                        first_norm(0)

            copy_v(0, 0)
            rounds(pool, NR, body)

            add_bo(1)
            first_norm(1)
            with pool.Fori(2, NC) as c:
                add_bo(c)
                second_norm(c - 2)
                first_norm(c)
            second_norm(NC - 2)
            second_norm(NC - 1)

        @block.tensor
        def _(pe):
            def scores(G, p, k, u):
                t, piece, lo, hi, heads = UNITS[u]
                bank = sbank[u % 3]
                for half in range(NH2):
                    if u == NEEDS[half]:
                        pe.wait_ge(stacked[half][p], k * 128 + 128)
                wait(pe, s["max_done"], G * NU + u - 2)
                for n, h in enumerate(heads):
                    at = n * (hi - lo)
                    m0, m1 = max(lo, P * t + WIN), hi
                    mm = pe.matmul(bank[:, at:at + hi - lo], QS[p][0:MR, t // NT, h, t % NT * P:t % NT * P + P],
                                   KS[p][0:MR, piece, h % 2, 0:hi - lo], start=True, stop=(m1 <= m0))
                    if m1 > m0:
                        mm = pe.matmul(bank[:, at + m0 - lo:at + hi - lo], idb[:],
                                       tri[:, m0 - P * t - WIN:m1 - P * t - WIN], start=False, stop=True)
                mm.then_inc(s["s_ready"], 1)

            def scoresT(G, p, k, i, h):
                qc, kt, q0 = SLOTS[i]
                u = i * HG + h
                if kt == 0 and h == 0:
                    pe.wait_ge(negmax[qc][p], k * 16 + 16)
                wait(pe, s["exp_done"], G * NST + (u - 2 if u >= 3 else LAST_OF[u] - NST + 1))
                pe.matmul(stbank[u % 3][:, 0:(qc + 1) * CH - q0],
                          KS[p][0:MR + 1, kt // NT, h % 2, kt % NT * P:kt % NT * P + P],
                          QS[p][0:MR + 1, qc, h, q0 - qc * CH:CH], start=True, stop=True).then_inc(s["st_ready"], 1)

            def weighted(G, p, i):
                qc, kt, q0 = SLOTS[i]
                if i == 0:
                    pe.wait_ge(s["v_copied"], G + 1)
                if kt == 0:
                    wait(pe, s["ot_done"], G * NH2 + qc)
                if i in MASKED:
                    pe.wait_ge(s["masked"], (G * len(MASKED) + MASKED.index(i) + 1) * 2)
                else:
                    pe.wait_ge(s["exp_done"], G * NST + (i + 1) * HG)
                for h in range(HG):
                    mm = pe.matmul(otbank[32 * h:32 * h + HD + 1, q0 - qc * CH:CH], VG[p][:, kt, h:VW:HG],
                                   PT[(p + i) % 2][:, h, 0:(qc + 1) * CH - q0], start=(kt == 0),
                                   stop=(i in HALF), skip_group_check=True)
                mm.then_inc(s["pv_done"], 1)

            def maxT(G, half):
                pe.wait_ge(s["both_max"], G * NH2 + half + 1)
                if half:
                    pe.wait_ge(s["mT_done"], G * NH2 + 1)
                else:
                    wait(pe, s["o_done"], NH2 * G - 1)
                pe.transpose(aux[0:HG * NT, 0:P], mx[:, 0, half].rearrange("p h t -> p (h t)"), ident[:])\
                  .then_inc(s["mT_ready"], 1)

            def outT(G, qc):
                pe.wait_ge(s["ot_done"], G * NH2 + qc + 1)
                if qc and not (isinstance(G, int) and G == NR - 1):
                    pe.wait_ge(s["mT_done"], (G + 1) * NH2 + NH2)
                else:
                    wait(pe, s["o_done"], G * NH2 + qc)
                for j in range(NT):
                    mm = pe.transpose(aux[:, j * P:j * P + P], OTs[:, j * P:j * P + P], ident[:])
                mm.then_inc(s["ott_ready"], 1)

            def project(c, p, k, last=False):
                pe.wait_ge(pre["x_split"], c + 1)
                for m in range(NM):
                    bank = pbank[m]
                    if m < 4:
                        wait(pe, pre["qk_f32"], c * 4 + m - 1)
                    else:
                        wait(pe, pre["v_done"], c * NT - NT + 2 * (m - 3))
                    for half in range(1 if m < 4 else 2):
                        n = 0
                        for w, xx in ((winh, xh[p]), (winh, xl[p]), (winl, xh[p])):
                            if w is winl and isinstance(c, int) and c == 0:
                                pe.wait_ge(pre["w_lo"], KD)
                            for kk in range(KD):
                                if m < 4:
                                    mm = pe.matmul(bank[:], w[:, kk, m * P:m * P + P], xx[:, kk, :],
                                                   start=(n == 0), stop=(n == 5))
                                else:
                                    lo = (2 * (m - 4) + half) * P
                                    mm = pe.matmul(bank[:, half * D:half * D + D], xx[:, kk, lo:lo + P],
                                                   w[:, kk, 2 * D:3 * D], start=(n == 0), stop=(n == 5))
                                n += 1
                    mm.then_inc(pre["proj_ready"], 1)
                    for u in first_scores(c, m):
                        scores(0, 0, 0, u)
                    if last and m == 1:
                        maxT(0, 0)

            pe.wait_ge(pre["w_hi"], KD)
            pe.wait_ge(pre["ident_done"], 1)
            pe.wait_ge(s["tri_done"], 2)
            rounds(pe, NC, project)
            pe.wait_ge(pre["qk_f32"], NC * 4)
            pe.wait_ge(pre["v_done"], NC * NT)
            pe.wait_ge(s["otb_zero"], 1)

            def step(c, what):
                if what == "ont":
                    pe.wait_ge(f["on_copied"], c + 1)
                    if isinstance(c, int) and c == 0:
                        pe.wait_ge(s["max_done"], NR * NU)
                    for k in range(KD):
                        wait(pe, f["x1_lo"], c * KD)
                        wait(pe, f["cT_done"], c)
                        for j in range(NT):
                            mm = pe.transpose(nbank(c)[k][:, j * P:j * P + P], On[:, j, k * P:k * P + P], ident[:])
                        mm.then_inc(f["ont_ready"], 1)
                elif what == "y":
                    pe.wait_ge(f["ont_done"], c * KD + KD)
                    for j in range(NT):
                        i = 0
                        for a, w in ((Oh, woh), (Ol, woh), (Oh, wol)):
                            for k in range(KD):
                                mm = pe.matmul(nbank(c)[j // 2][:, (j % 2) * D:(j % 2) * D + D],
                                               a[:, k, j * P:j * P + P], w[:, k, :], start=(i == 0), stop=(i == 5))
                                i += 1
                    mm.then_inc(f["y_ready"], 1)
                elif what == "x1t":
                    pe.wait_ge(f["x1_done"], c * NT + NT)
                    for k in range(KD):
                        for j in range(NT):
                            mm = pe.transpose(nbank(c)[k][:, j * P:j * P + P], x1c[:, j, k * P:k * P + P], ident[:])
                        mm.then_inc(f["x1t_ready"], 1)
                elif what == "logits":
                    pe.wait_ge(f["x1_lo"], c * KD + KD)
                    for j in range(NT):
                        i = 0
                        for a, w in ((x1h, rwh), (x1l, rwh), (x1h, rwl)):
                            for k in range(KD):
                                mm = pe.matmul(nbank(c)[0][:, j * NE:j * NE + NE],
                                               a[:, k, bass.ds(c * CH + j * P, P)], w[:, k, :],
                                               start=(i == 0), stop=(i == 5))
                                i += 1
                    mm.then_inc(f["lg_ready"], 1)
                elif what == "cT":
                    pe.wait_ge(f["c_done"], c + 1)
                    for j in range(NT):
                        mm = pe.transpose(nbank(c)[0][0:NE, j * P:j * P + P], cw[:, j, :], ident[:])
                    mm.then_inc(f["cT_ready"], 1)

            pe.wait_ge(f["w_loaded"], 64)
            pe.wait_ge(f["rw_lo"], 2)

            def body(G, p, k, last=False):
                def some_scores(units):
                    for u, ahead in units:
                        if not ahead:
                            scores(G, p, k, u)
                        elif not last:
                            scores(G + 1, 1 - p, k + p, u)

                for i in range(NSL):
                    rest = share(i)
                    for h in range(HG):
                        scoresT(G, p, k, i, h)
                        some_scores(rest[h:h + 1] if h < HG - 1 else ())
                    if i:
                        weighted(G, p, i - 1)
                    some_scores(rest[HG - 1:])
                    if i == MAXT[1]:
                        maxT(G, 1)
                    if i == OTT[1] and not (isinstance(G, int) and G == 0):
                        outT(G - 1, 1)
                    if i == OTT[0]:
                        outT(G, 0)
                    if i == MAXT[0] and not last:
                        maxT(G + 1, 0)
                    if last:
                        for what in STEPS0.get(i, ()):
                            step(0, what)
                weighted(G, p, NSL - 1)

            rounds(pe, NR, body)
            outT(NR - 1, 1)

            def up(t, n):
                N = t * NX + n
                for bank, w, free, ready in ((gbank[n % 2], "g", "silu_done", "g_ready"),
                                             (ubank[n % 2], "u", "h_done", "u_ready")):
                    wait(pe, f[free], N - 1)
                    i = 0
                    for ww, xx in ((wh[w], x1h), (wh[w], x1l), (wl[w], x1h)):
                        for k in range(KD):
                            mm = pe.matmul(bank[:], ww[:, k, n, :], xx[:, k, bass.ds(t * CH, CH)],
                                           start=(i == 0), stop=(i == 5))
                            i += 1
                    mm.then_inc(f[ready], 1)

            def down(t, n):
                pe.wait_ge(f["lo_done"], t * NX + n + 1)
                if n == 0:
                    wait(pe, f["z2_done"], t * NT)
                for j in range(NT):
                    y = ybank[j // 2][:, (j % 2) * D:(j % 2) * D + D]
                    for i, (a, w) in enumerate(((hh, wh["d"]), (hh, wl["d"]), (hl, wh["d"]))):
                        mm = pe.matmul(y, a[n % NHB][:, j * P:j * P + P], w[:, n, :],
                                       start=(n == 0 and i == 0 and j % 2 == 0),
                                       stop=(n == NX - 1 and i == 2), skip_group_check=True)
                mm.then_inc(f["down_done"], 1)

            step(0, "cT")
            pe.wait_ge(f["cT_done"], 1)
            pe.wait_ge(s["exp_done"], NR * NST)
            pe.wait_ge(s["max_done"], NR * NU)
            pe.wait_ge(s["o_done"], NR * NH2)
            pe.wait_ge(s["w_lo"], NX * 3)

            def chunk(t, first=False, last=False):
                for n in range(NX):
                    up(t, n)
                    if n >= LAG:
                        down(t, n - LAG)
                    elif not first:
                        down(t - 1, NX - LAG + n)
                    if n in STEPS and not last:
                        step(t + 1, STEPS[n])

            chunk(0, first=True)
            with pe.Fori(1, NC - 1) as t:
                chunk(t)
            chunk(NC - 1, last=True)
            for n in range(NX - LAG, NX):
                down(NC - 1, n)

        @block.scalar
        def _(act):
            def load_x(c, p):
                act.wait_ge(pre["x_split"], c - 1)
                act.dma_start(xf[p][:], xT[:, bass.ds(c * CH, CH)].rearrange("(k p) t -> p k t", p=P))\
                   .then_inc(x_loaded[p], 16)

            def hi_x(c, p, k):
                act.wait_ge(x_loaded[p], k * 16 + 16)
                wait(act, pre["proj_ready"], (c - 1) * NM)
                act.copy(xh[p][:], xf[p][:]).then_inc(pre["x_hi"], 1)

            hi_x(0, 0, 0)
            for k in range(KD):
                act.wait_ge(pre[f"w_loaded{k}"], 16)
                act.mul(winh[:, k, :], stage[:, k, :], WSC).then_inc(pre["w_hi"], 1)
            act.wait_ge(pre["b_loaded"], 32)
            act.mul(bqs[:, 0:2], bqk[:, 0:2], HD ** -0.5).then_inc(pre["bias_done"], 1)
            act.copy(bqs[:, 2:4], bqk[:, 2:4]).then_inc(pre["bias_done"], 1)
            act.wait_ge(pre["bias_done"], 2)

            def mT_copy(G, p, k, half):
                act.wait_ge(s["mT_ready"], G * NH2 + half + 1)
                if not (isinstance(G, int) and G == 0):
                    act.wait_ge(negmax[half][1 - p], (k + p) * 16)
                act.mul(mT[half][:], aux[0:HG * NT, 0:P], -1.0).then_inc(s["mT_done"], 1)

            def project(c, p, k, last=False):
                if not (isinstance(c, int) and c >= NC - 2):
                    load_x(c + 2, p)
                if not last:
                    hi_x(c + 1, 1 - p, k + p)
                for m in range(4):
                    act.wait_ge(pre["proj_ready"], c * NM + m + 1)
                    wait(act, pre["qk_lo"], c * 4 - 4 + m + 1)
                    scale = (HD ** -0.5 if m < 2 else 1.0) / WSC
                    act.activation(qkf[m][:], pbank[m][:], ACT.Identity, bias=bqs[:, m:m + 1], scale=scale)\
                       .then_inc(pre["qk_f32"], 1)
                    if last and m == 1:
                        mT_copy(0, 0, 0, 0)

            rounds(act, NC, project)

            def split_hi(n, p, k):
                act.wait_ge(raw_loaded[p], (k + 1) * 16 * NRAW)
                for src, dst in zip(parts(raw[p]), split_of(wh, n)):
                    act.mul(dst, src, WSC).then_inc(s["w_hi"], 1)

            def exp(G, p, i, h):
                qc, kt, q0 = SLOTS[i]
                u = i * HG + h
                act.wait_ge(s["st_ready"], G * NST + u + 1)
                if h == 0:
                    wait(act, s["pv_done"], G * NSL + i - 1)
                w = (qc + 1) * CH - q0
                act.activation(PT[(p + i) % 2][:, h, 0:w], stbank[u % 3][:, 0:w], ACT.Exp)\
                   .then_inc(s["exp_done"], 1)

            def out_copy(G, qc):
                act.wait_ge(s["pv_done"], G * NSL + HALF[qc] + 1)
                wait(act, s["ott_ready"], G * NH2 + qc)
                act.copy(OTs[:], otbank[:]).then_inc(s["ot_done"], 1)

            act.wait_ge(f["w_loaded"], 64)
            act.mul(rwh[:], rwf[:], WSC).then_inc(f["rw_hi"], 1)
            act.mul(woh[:], wo[:], WSC).then_inc(f["rw_hi"], 1)

            def step(c, what):
                if what == "on":
                    wait(act, f["ont_ready"], c * KD)
                    for j in range(NT):
                        mm = act.copy(On[:, j, :].rearrange("p (g n) -> p g n", g=NG), kept(c)[:, :, j, :])
                    mm.then_inc(f["on_copied"], 1)
                elif what == "ont":
                    for k in range(KD):
                        act.wait_ge(f["ont_ready"], c * KD + k + 1)
                        wait(act, f["y_ready"], c)
                        act.copy(Oh[:, k, :], nbank(c)[k][:]).then_inc(f["ont_hi"], 1)
                elif what == "x1t":
                    if isinstance(c, int) and c == 0:
                        act.wait_ge(s["v_copied"], NR)
                    for k in range(KD):
                        act.wait_ge(f["x1t_ready"], c * KD + k + 1)
                        act.copy(x1h[:, k, bass.ds(c * CH, CH)], nbank(c)[k][:]).then_inc(f["x1_hi"], 1)
                elif what == "logits":
                    act.wait_ge(f["lg_ready"], c + 1)
                    wait(act, f["c_done"], c)
                    act.activation(th[:].rearrange("p j e -> p (j e)"), nbank(c)[0][:, 0:NT * NE], ACT.Tanh,
                                   scale=0.5 / WSC).then_inc(f["th_done"], 1)
                elif what == "cT":
                    act.wait_ge(f["cT_ready"], c + 1)
                    wait(act, f["cT_written"], c * 16)
                    act.copy(cT[:], nbank(c)[0][0:NE, :]).then_inc(f["cT_done"], 1)

            def body(G, p, k, last=False):
                for i in range(NSL):
                    for h in range(HG):
                        exp(G, p, i, h)
                    if i == 0 and not (isinstance(G, int) and G == 0):
                        out_copy(G - 1, NH2 - 1)
                    if i == HALF[0] + 1:
                        out_copy(G, 0)
                    if i == 1 and isinstance(G, int) and G == 0:
                        act.wait_ge(pre["qk_lo"], NC * 4)
                        act.wait_ge(pre["proj_ready"], NC * NM)
                        for q in range(2):
                            act.wait_ge(qk_written[q], 128 * (NC // 2))
                        for n in range(NSH):
                            split_hi(n, n, 0)
                    if i == HALF[0]:
                        split_hi(G + NSH, p, k + 1)
                    if i == MAXT[1]:
                        mT_copy(G, p, k, 1)
                    if i == MAXT[0] and not last:
                        mT_copy(G + 1, 1 - p, k + p, 0)
                    if last:
                        for what in STEPS0.get(i, ()):
                            step(0, what)

            rounds(act, NR, body)
            out_copy(NR - 1, NH2 - 1)

            def silu(t, n):
                N = t * NX + n
                act.wait_ge(f["g_ready"], N + 1)
                wait(act, f["h_done"], N - 1)
                act.activation(sg[n % 2][:], gbank[n % 2][:], ACT.Silu, scale=1.0 / WSC).then_inc(f["silu_done"], 1)

            def high(t, n):
                N = t * NX + n
                act.wait_ge(f["h_done"], N + 1)
                wait(act, f["down_done"], N - NHB + 1)
                act.copy(hh[n % NHB][:], hf[n % 2][:]).then_inc(f["hi_done"], 1)

            step(0, "cT")

            def chunk(t, last=False):
                for n in range(NX):
                    silu(t, n)
                    high(t, n)
                    if n in STEPS and not last:
                        step(t + 1, STEPS[n])

            chunk(0)
            with act.Fori(1, NC - 1) as t:
                chunk(t)
            chunk(NC - 1, last=True)

        @block.vector
        def _(dve):
            for a in (QS[0], QS[1]):
                dve.memset(a[:], 0.0).then_inc(s["stack_zero"], 1)
            for k in range(KD):
                dve.wait_ge(pre["w_hi"], k + 1)
                dve.scalar_tensor_tensor(winl[:, k, :], stage[:, k, :], WSC, winh[:, k, :], op0=ALU.mult,
                                         op1=ALU.subtract).then_inc(pre["w_lo"], 1)
            dve.wait_ge(pre["b_loaded"], 32)
            dve.wait_ge(s["stack_zero"], 4)
            for a in KS:
                dve.memset(a[96:P], 1.0).then_inc(s["stack_const"], 2)

            def smax(G, p, u):
                t, piece, lo, hi, heads = UNITS[u]
                n, w = len(heads), hi - lo
                dve.wait_ge(s["s_ready"], G * NU + u + 1)
                if u in (0, SECOND):
                    wait(dve, s["mT_ready"], G * NH2 - 1 + (u == SECOND))
                dve.tensor_reduce(mx[:, piece, t // NT, heads[0]:heads[0] + n, t % NT],
                                  sbank[u % 3][:, 0:n * w].rearrange("p (h k) -> p h k", h=n),
                                  AX.X, ALU.max).then_inc(s["max_done"], 1)

            def both(G, half):
                dve.wait_ge(s["max_done"], G * NU + (NU if half else SECOND))
                a, b = (mx[:, n, half, :, 0 if half else NT - 1:NT] for n in range(2))
                dve.tensor_tensor(a, a, b, op=ALU.max).then_inc(s["both_max"], 1)

            def normal(G, qc):
                n = G * NH2 + qc
                dve.wait_ge(s["ott_ready"], n + 1)
                o = aux[:].rearrange("p (j h e) -> p j h e", j=NT, e=32)
                dve.reciprocal(rec[:].unsqueeze(3), o[:, :, :, HD:HD + 1]).then_inc(s["rec_done"], 1)
                dve.wait_ge(s["rec_done"], n + 1)
                dst = o_all[:, qc, bass.ds(G, 1), :, :].squeeze(1)
                for j in range(NT):
                    mm = dve.tensor_tensor(dst[:, j, :].rearrange("p (h d) -> p h d", d=HD), o[:, j, :, 0:HD],
                                           rec[:, j, :].unsqueeze(2).to_broadcast([P, HG, HD]), op=ALU.mult)
                mm.then_inc(s["o_done"], 1)

            def split_lo(n, p):
                for i, (src, hi_, dst) in enumerate(zip(parts(raw[p]), split_of(wh, n), split_of(wl, n))):
                    dve.wait_ge(s["w_hi"], 3 * n + i + 1)
                    dve.scalar_tensor_tensor(dst, src, WSC, hi_, op0=ALU.mult, op1=ALU.subtract)\
                       .then_inc(s["w_lo"], 1)

            def project(c, p, k, last=False):
                if last:
                    both(0, 0)
                for m in range(NM):
                    if m < 4:
                        dve.wait_ge(pre["qk_f32"], c * 4 + m + 1)
                        if m == 0:
                            wait(dve, qk_written[p], k * 128)
                        dve.tensor_copy(qk16[p][:, 0, m, :], qkf[m][:]).then_inc(pre["qk_hi"], 1)
                    else:
                        dve.wait_ge(pre["proj_ready"], c * NM + m + 1)
                        for n in range(2):
                            tile = p * NT + 2 * (m - 4) + n
                            dve.scalar_tensor_tensor(v_all[:, bass.ds(k * NG, NG), tile, 0:HG * HD],
                                                     pbank[m][:, n * D:n * D + D]
                                                     .rearrange("p (g n) -> p g n", g=NG),
                                                     1.0 / WSC, bv[:], op0=ALU.mult, op1=ALU.add)\
                               .then_inc(pre["v_done"], 1)
                    for u in first_scores(c, m):
                        smax(0, 0, u)

            rounds(dve, NC, project)
            dve.memset(otbank[:], 0.0).then_inc(s["otb_zero"], 1)

            for n, (lo, w, hi) in enumerate(((rwl, rwf, rwh), (wol, wo, woh))):
                dve.wait_ge(f["rw_hi"], n + 1)
                dve.scalar_tensor_tensor(lo[:], w[:], WSC, hi[:], op0=ALU.mult, op1=ALU.subtract)\
                   .then_inc(f["rw_lo"], 1)
            dve.wait_ge(f["consts"], 3)

            def variance(w, c, z_done, per, stats_done, var_done):
                for j in range(NT):
                    dve.wait_ge(z_done, c * per + j // (NT // per) + 1)
                    dve.bn_stats(st[w][:, j, :], zz[w][:, j, :]).then_inc(stats_done, 1)
                for j in range(NT):
                    dve.wait_ge(stats_done, c * NT + j + 1)
                    settle(dve, s["settled"])
                    dve.bn_aggr(mv[w][:, j, :], st[w][:, j, :]).then_inc(var_done, 1)

            def norm(w, dst, ready):
                for j in range(NT):
                    dve.tensor_scalar(dst[:, j, :], zz[w][:, j, :], mv[w][:, j, 0:1], rstd[w][:, j:j + 1],
                                      op0=ALU.subtract, op1=ALU.mult).then_inc(ready, 1)

            def step(c, what):
                if what == "ont":
                    for k in range(KD):
                        dve.wait_ge(f["ont_hi"], c * KD + k + 1)
                        dve.tensor_tensor(Ol[:, k, :], nbank(c)[k][:], Oh[:, k, :], op=ALU.subtract)\
                           .then_inc(f["ont_done"], 1)
                elif what == "y":
                    dve.wait_ge(f["y_ready"], c + 1)
                    dve.wait_ge(f["xb_done"], c + 1)
                    for i in range(2):
                        dve.scalar_tensor_tensor(zz[0][:, 2 * i:2 * i + 2, :].rearrange("p j n -> p (j n)"),
                                                 nbank(c)[i][:], 1.0 / WSC,
                                                 xb[:, 2 * i:2 * i + 2, :].rearrange("p j n -> p (j n)"),
                                                 op0=ALU.mult, op1=ALU.add).then_inc(f["z_done"], 1)
                elif what == "var":
                    variance(0, c, f["z_done"], 2, f["stats_done"], f["var_done"])
                elif what == "norm":
                    dve.wait_ge(f["rstd_done"], c + 1)
                    wait(dve, f["x1_kept"], c)
                    norm(0, x1c, f["x1_done"])
                elif what == "x1t":
                    for k in range(KD):
                        dve.wait_ge(f["x1_hi"], c * KD + k + 1)
                        dve.tensor_tensor(x1l[:, k, bass.ds(c * CH, CH)], nbank(c)[k][:],
                                          x1h[:, k, bass.ds(c * CH, CH)], op=ALU.subtract).then_inc(f["x1_lo"], 1)
                elif what[:-1] == "route":
                    route(c, int(what[-1]))

            FROM = [0, 7, 13, 20, 22, 30]

            def route(c, part):
                done = [FROM[part]]

                def link(ins):
                    done[0] += 1
                    ins.then_inc(f["route_step"], 1)
                    dve.wait_ge(f["route_step"], c * FROM[-1] + done[0])

                s4 = sc[:].rearrange("p t (g e) -> p t g e", e=4)
                pairs = [(a, b) for a in range(4) for b in range(a + 1, 4)]
                if part == 0:
                    dve.wait_ge(f["th_done"], c + 1)
                    link(dve.tensor_scalar(th[:], th[:], 0.5, 0.5, op0=ALU.mult, op1=ALU.add))
                    link(dve.tensor_tensor(sc[:], th[:], eb[:].unsqueeze(1).to_broadcast([P, NT, NE]), op=ALU.add))
                    link(dve.tensor_tensor(pr[0][:], s4[:, :, :, 0], s4[:, :, :, 1], op=ALU.add))
                    for a, b in pairs[1:3]:
                        link(dve.tensor_tensor(pr[1][:], s4[:, :, :, a], s4[:, :, :, b], op=ALU.add))
                        link(dve.tensor_tensor(pr[0][:], pr[0][:], pr[1][:], op=ALU.max))
                elif part == 1:
                    for a, b in pairs[3:]:
                        link(dve.tensor_tensor(pr[1][:], s4[:, :, :, a], s4[:, :, :, b], op=ALU.add))
                        link(dve.tensor_tensor(pr[0][:], pr[0][:], pr[1][:], op=ALU.max))
                elif part == 2:
                    g4 = pr[0][:]
                    gg, ge = gt[:, :, 0:4, 0:4], eq[:, :, 0:4, 0:4]
                    one = g4.unsqueeze(2).to_broadcast([P, NT, 4, 4])
                    two = g4.unsqueeze(3).to_broadcast([P, NT, 4, 4])
                    link(dve.tensor_tensor(gg, one, two, op=ALU.is_gt))
                    link(dve.tensor_tensor(ge, one, two, op=ALU.is_equal))
                    link(dve.tensor_tensor(ge, ge, lower[:, 0:4, 0:4].unsqueeze(1).to_broadcast([P, NT, 4, 4]),
                                           op=ALU.mult))
                    link(dve.tensor_tensor(gg, gg, ge, op=ALU.add))
                    link(dve.tensor_reduce(rk[:], gg, AX.X, ALU.add))
                    link(dve.tensor_scalar(rk[:], rk[:], 2.0, None, op0=ALU.is_lt))
                    v4 = vm[:].rearrange("p t (g e) -> p t g e", e=4)
                    link(dve.tensor_tensor(v4, s4, rk[:].unsqueeze(3).to_broadcast([P, NT, 4, 4]), op=ALU.mult))
                elif part == 3:
                    one = vm[:].unsqueeze(2).to_broadcast([P, NT, NE, NE])
                    two = vm[:].unsqueeze(3).to_broadcast([P, NT, NE, NE])
                    link(dve.tensor_tensor(gt[:], one, two, op=ALU.is_gt))
                    link(dve.tensor_tensor(eq[:], one, two, op=ALU.is_equal))
                else:
                    link(dve.tensor_tensor(eq[:], eq[:], lower[:].unsqueeze(1).to_broadcast([P, NT, NE, NE]),
                                           op=ALU.mult))
                    link(dve.tensor_tensor(gt[:], gt[:], eq[:], op=ALU.add))
                    link(dve.tensor_reduce(rank[:], gt[:], AX.X, ALU.add))
                    link(dve.scalar_tensor_tensor(vm[:], rank[:], float(TOPK), th[:], op0=ALU.is_lt, op1=ALU.mult))
                    link(dve.tensor_reduce(tot[:], vm[:], AX.X, ALU.add))
                    link(dve.tensor_scalar(tot[:], tot[:], 1e-20, None, op0=ALU.add))
                    link(dve.reciprocal(tot[:], tot[:]))
                    link(dve.tensor_tensor(vm[:], vm[:], tot[:].unsqueeze(2).to_broadcast([P, NT, NE]),
                                           op=ALU.mult))
                    wait(dve, f["cT_ready"], c)
                    dve.tensor_scalar(cw[:], vm[:], 2.5, None, op0=ALU.mult).then_inc(f["c_done"], 1)
                assert done[0] == (FROM + [0])[part + 1], done

            def body(G, p, k, last=False):
                for i in range(NSL):
                    for u, ahead in share(i):
                        if not ahead:
                            smax(G, p, u)
                        elif not last:
                            smax(G + 1, 1 - p, u)
                    if i == MAXT[1]:
                        both(G, 1)
                    if i == OTT[1] and not (isinstance(G, int) and G == 0):
                        normal(G - 1, 1)
                    if i == OTT[0]:
                        normal(G, 0)
                    if i == MAXT[0] - 1 and not last:
                        both(G + 1, 0)
                    if i == 2 and isinstance(G, int) and G == 0:
                        for n in range(NSH):
                            split_lo(n, n)
                    if i == HALF[0] + 1:
                        split_lo(G + NSH, p)
                    if last:
                        for what in STEPS0.get(i, ()):
                            step(0, what)

            rounds(dve, NR, body)
            normal(NR - 1, NH2 - 1)

            def gated(t, n):
                N = t * NX + n
                dve.wait_ge(f["silu_done"], N + 1)
                if n >= NSH:
                    e = n - NSH
                    dve.wait_ge(c_loaded[e % NCB], (t * (NE // NCB) + e // NCB) * 16 + 16)
                    dve.tensor_tensor(sg[n % 2][:], sg[n % 2][:], cb[e % NCB][:], op=ALU.mult)\
                       .then_inc(f["sc_done"], 1)
                    dve.wait_ge(f["sc_done"], t * NE + e + 1)
                dve.wait_ge(f["u_ready"], N + 1)
                wait(dve, f["lo_done"], N - 1)
                wait(dve, f["hi_done"], N - 1)
                dve.scalar_tensor_tensor(hf[n % 2][:], ubank[n % 2][:], 1.0 / WSC, sg[n % 2][:],
                                         op0=ALU.mult, op1=ALU.mult).then_inc(f["h_done"], 1)

            def low(t, n):
                N = t * NX + n
                dve.wait_ge(f["hi_done"], N + 1)
                wait(dve, f["down_done"], N - NHB + 1)
                dve.tensor_tensor(hl[n % NHB][:], hf[n % 2][:], hh[n % NHB][:], op=ALU.subtract)\
                   .then_inc(f["lo_done"], 1)

            def residual(t):
                dve.wait_ge(f["down_done"], t * NX + NX)
                dve.wait_ge(f["x1_kept"], t + 1)
                for j in range(NT):
                    y = ybank[j // 2][:, (j % 2) * D:(j % 2) * D + D].rearrange("p (g n) -> p g n", g=NG)
                    dve.scalar_tensor_tensor(zz[1][:, j, :].rearrange("p (g n) -> p g n", g=NG), y, 1.0 / WSC,
                                             kept(t)[:, :, j, :], op0=ALU.mult, op1=ALU.add)\
                       .then_inc(f["z2_done"], 1)

            def finish(t, n):
                if n == LAG:
                    residual(t)
                elif n == LAG + 1:
                    variance(1, t, f["z2_done"], NT, f["stats2_done"], f["var2_done"])
                elif n == LAG + 3:
                    dve.wait_ge(f["rstd2_done"], t + 1)
                    wait(dve, f["out_written"], t * 16)
                    norm(1, oo, f["out_ready"])

            def chunk(t, first=False, last=False):
                for n in range(NX):
                    if not first:
                        finish(t - 1, n)
                    gated(t, n)
                    low(t, n)
                    if n in STEPS and not last:
                        step(t + 1, STEPS[n])

            chunk(0, first=True)
            with dve.Fori(1, NC - 1) as t:
                chunk(t)
            chunk(NC - 1, last=True)
            for n in range(NX):
                finish(NC - 1, n)


def halves_first(a):
    return a.reshape(B, NH2, CH, D).swapaxes(0, 1).reshape(T, D)


def kernel(**inputs):
    import numpy as np
    import concourse.bacc as bacc
    from concourse.bass_utils import run_bass_kernel_spmd

    g = {k: np.asarray(v) for k, v in inputs.items()}
    x = g["L0_attn_x"].reshape(T, D)

    def by_dim(a):
        return a.reshape(NG, HG, HD, *a.shape[1:]).swapaxes(1, 2).reshape(a.shape)

    def by_pair(a):
        return a.reshape(NG, 2, 2, HD, *a.shape[1:]).swapaxes(2, 3).reshape(a.shape)

    w, b = g["L0_attn_in_proj_w"].reshape(3, D, D), g["L0_attn_in_proj_b"].reshape(3, D)
    arrays = {
        "x": halves_first(x),
        "xT": x.T,
        "winT": np.concatenate([by_pair(w[0]), by_pair(w[1]), by_dim(w[2])]).T,
        "bqkT": np.concatenate([by_pair(b[0]), by_pair(b[1])]).reshape(2 * KD, P).T,
        "bvr": by_dim(b[2]),
        "woutT": g["L0_attn_out_proj_w"].T,
        "bout": g["L0_attn_out_proj_b"],
        "rwT": g["L0_ffn_router_weight"].T,
        "ebias": g["L0_ffn_e_bias"],
        "gwT": g["L0_ffn_gate_w"].transpose(2, 0, 1),
        "uwT": g["L0_ffn_up_w"].transpose(2, 0, 1),
        "dwT": g["L0_ffn_down_w"].transpose(2, 0, 1),
        "sgT": g["L0_ffn_sh_gate_w"].T,
        "suT": g["L0_ffn_sh_up_w"].T,
        "sdT": g["L0_ffn_sh_down_w"].T,
    }
    nc = bacc.Bacc("TRN2", target_bir_lowering=False, num_devices=1)
    ins = {}
    for name, a in list(arrays.items()):
        a = np.ascontiguousarray(a)
        arrays[name] = a
        ins[name] = nc.dram_tensor(name, a.shape, mybir.dt.from_np(a.dtype), kind="ExternalInput").ap()
    out = nc.dram_tensor("out", (T, D), F32, kind="ExternalOutput").ap()
    attention_moe(nc, **ins, out=out)
    r = run_bass_kernel_spmd(nc, [arrays], core_ids=[0])
    return r.results[0]["out"].reshape(NH2, B, CH, D).swapaxes(0, 1).reshape(B, S, D)
```
